# Optimizing a Trainium2 kernel written in Bass

```python
import numpy as np
import jax
import jax.numpy as jnp

def _softmax(x, axis=-1):
    return jax.nn.softmax(x, axis=axis)

def _gelu(x):
    return jax.nn.gelu(x, approximate=True)

def _silu(x):
    return jax.nn.silu(x)

def _sigmoid(x):
    return jax.nn.sigmoid(x)

def _layernorm(x, axis=-1, eps=1e-05):
    m = jnp.mean(x, axis=axis, keepdims=True)
    v = jnp.var(x, axis=axis, keepdims=True)
    return (x - m) / jnp.sqrt(v + eps)

def _scatter_add(tgt, idx, src, axis=0):
    return tgt.at[idx].add(src)

def _segment_sum(src, seg, n):
    return jax.ops.segment_sum(src, seg, n)
kernel_name = 'mk_gnn_resnorm_d1_gnn_r8_4d3c3c'

def setup_inputs(seed: int=0):
    np.random.seed(seed)
    _w = jnp.asarray

    def _rec_inputs():
        import jax
        import jax.numpy as jnp
        _gk = jax.random.key(seed)
        x = -0.0002928 + 1 * jax.random.normal(jax.random.fold_in(_gk, 1), (6250, 256), jnp.float32)
        _s = jax.random.randint(jax.random.fold_in(_gk, 2), (100000,), 0, 6250, jnp.int32)
        _d = jax.random.randint(jax.random.fold_in(_gk, 3), (100000,), 0, 6250, jnp.int32)
        _loop = jnp.arange(6250, dtype=jnp.int32)
        src = jnp.concatenate([_s, _d, _loop])
        dst = jnp.concatenate([_d, _s, _loop])
        _o = jnp.argsort(dst, stable=True)
        src = src[_o]
        dst = dst[_o]
        return (x, src, dst)
    x, src, dst = _rec_inputs()

    def _L0_gnn_setup():
        import jax, jax.numpy as jnp
        import numpy as np
        N_NODES = 2048
        N_EDGES = 32768
        D_IN = 256
        D = 256
        H = 512
        E = 64
        TOP_K = 2
        CAP = 1024
        BN_EPS = 1e-05

        def _moe_ff(x, Wg, bg, w1, b1, w2, b2):
            N = x.shape[0]
            logits = x @ Wg + bg
            vals, idx = jax.lax.top_k(logits, TOP_K)
            gates = jax.nn.softmax(vals, axis=-1)
            e_flat = idx.reshape(-1)
            g_flat = gates.reshape(-1)
            tok = jnp.arange(N * TOP_K) // TOP_K
            order = jnp.argsort(e_flat)
            e_s, tok_s, g_s = (e_flat[order], tok[order], g_flat[order])
            counts = jnp.bincount(e_flat, length=E)
            offs = jnp.concatenate([jnp.zeros((1,), counts.dtype), jnp.cumsum(counts)[:-1]])
            rank = jnp.arange(N * TOP_K) - offs[e_s]
            valid = rank < CAP
            slot = jnp.where(valid, e_s * CAP + rank, E * CAP)
            buf = jnp.zeros((E * CAP + 1, D), x.dtype).at[slot].set(x[tok_s])
            h = buf[:E * CAP].reshape(E, CAP, D)
            h1 = jax.nn.gelu(jnp.einsum('ecd,edh->ech', h, w1) + b1[:, None, :], approximate=False)
            h2 = jnp.einsum('ech,ehd->ecd', h1, w2) + b2[:, None, :]
            out_buf = h2.reshape(E * CAP, D)
            y_s = jnp.where(valid[:, None], out_buf[jnp.minimum(slot, E * CAP - 1)], 0.0)
            return jnp.zeros((N, D), x.dtype).at[tok_s].add(g_s[:, None] * y_s)

        def _forward(feats, W_gc, b_gc, W_res, b_res, Wg, bg, w1, b1, w2, b2, gamma, beta, src, dst):
            n = feats.shape[0]
            ones = jnp.ones((src.shape[0],), feats.dtype)
            deg_out = jnp.clip(jax.ops.segment_sum(ones, src, num_segments=n), 1.0)
            deg_in = jnp.clip(jax.ops.segment_sum(ones, dst, num_segments=n), 1.0)
            h = feats * jax.lax.rsqrt(deg_out)[:, None]
            m = jax.ops.segment_sum(h[src], dst, num_segments=n) * jax.lax.rsqrt(deg_in)[:, None]
            gc = m @ W_gc + b_gc
            x = gc + (feats @ W_res + b_res)
            core = _moe_ff(x, Wg, bg, w1, b1, w2, b2)
            y = x + core
            mean = jnp.mean(y, axis=0)
            var = jnp.mean((y - mean) ** 2, axis=0)
            return (y - mean) * jax.lax.rsqrt(var + BN_EPS) * gamma + beta
        key = jax.random.key(seed)
        ks = jax.random.split(key, 16)
        s = lambda d: 1.0 / np.sqrt(d)
        inp = {'feats': jax.random.normal(ks[0], (N_NODES, D_IN), jnp.float32), 'W_gc': jax.random.normal(ks[1], (D_IN, D), jnp.float32) * s(D_IN), 'b_gc': jnp.zeros((D,), jnp.float32), 'W_res': jax.random.normal(ks[2], (D_IN, D), jnp.float32) * s(D_IN), 'b_res': jnp.zeros((D,), jnp.float32), 'Wg': jax.random.normal(ks[3], (D, E), jnp.float32) * s(D), 'bg': jnp.zeros((E,), jnp.float32), 'w1': jax.random.normal(ks[4], (E, D, H), jnp.float32) * s(D), 'b1': jnp.zeros((E, H), jnp.float32), 'w2': jax.random.normal(ks[5], (E, H, D), jnp.float32) * s(H), 'b2': jnp.zeros((E, D), jnp.float32), 'gamma': jnp.ones((D,), jnp.float32), 'beta': jnp.zeros((D,), jnp.float32), 'src': jax.random.randint(ks[6], (N_EDGES,), 0, N_NODES), 'dst': jax.random.randint(ks[7], (N_EDGES,), 0, N_NODES)}
        return inp
    _L0_gnn_all = _L0_gnn_setup()
    _L0_gnn_in = {k: v for k, v in _L0_gnn_all.items() if k in ('W_gc', 'b_gc', 'W_res', 'b_res', 'Wg', 'bg', 'w1', 'b1', 'w2', 'b2', 'gamma', 'beta')}
    del _L0_gnn_all
    return {'x': x, 'src': src, 'dst': dst, 'L0_gnn_W_gc': _L0_gnn_in['W_gc'], 'L0_gnn_b_gc': _L0_gnn_in['b_gc'], 'L0_gnn_W_res': _L0_gnn_in['W_res'], 'L0_gnn_b_res': _L0_gnn_in['b_res'], 'L0_gnn_Wg': _L0_gnn_in['Wg'], 'L0_gnn_bg': _L0_gnn_in['bg'], 'L0_gnn_w1': _L0_gnn_in['w1'], 'L0_gnn_b1': _L0_gnn_in['b1'], 'L0_gnn_w2': _L0_gnn_in['w2'], 'L0_gnn_b2': _L0_gnn_in['b2'], 'L0_gnn_gamma': _L0_gnn_in['gamma'], 'L0_gnn_beta': _L0_gnn_in['beta']}

def reference(x, src, dst, L0_gnn_W_gc, L0_gnn_b_gc, L0_gnn_W_res, L0_gnn_b_res, L0_gnn_Wg, L0_gnn_bg, L0_gnn_w1, L0_gnn_b1, L0_gnn_w2, L0_gnn_b2, L0_gnn_gamma, L0_gnn_beta):
    import jax
    import jax.numpy as jnp

    def _L0_gnn_ref(feats, W_gc, b_gc, W_res, b_res, Wg, bg, w1, b1, w2, b2, gamma, beta, src, dst):
        import jax, jax.numpy as jnp
        import numpy as np
        N_NODES = 2048
        N_EDGES = 32768
        D_IN = 256
        D = 256
        H = 512
        E = 64
        TOP_K = 2
        CAP = 1024
        BN_EPS = 1e-05

        def _moe_ff(x, Wg, bg, w1, b1, w2, b2):
            N = x.shape[0]
            logits = x @ Wg + bg
            vals, idx = jax.lax.top_k(logits, TOP_K)
            gates = jax.nn.softmax(vals, axis=-1)
            e_flat = idx.reshape(-1)
            g_flat = gates.reshape(-1)
            tok = jnp.arange(N * TOP_K) // TOP_K
            order = jnp.argsort(e_flat)
            e_s, tok_s, g_s = (e_flat[order], tok[order], g_flat[order])
            counts = jnp.bincount(e_flat, length=E)
            offs = jnp.concatenate([jnp.zeros((1,), counts.dtype), jnp.cumsum(counts)[:-1]])
            rank = jnp.arange(N * TOP_K) - offs[e_s]
            valid = rank < CAP
            slot = jnp.where(valid, e_s * CAP + rank, E * CAP)
            buf = jnp.zeros((E * CAP + 1, D), x.dtype).at[slot].set(x[tok_s])
            h = buf[:E * CAP].reshape(E, CAP, D)
            h1 = jax.nn.gelu(jnp.einsum('ecd,edh->ech', h, w1) + b1[:, None, :], approximate=False)
            h2 = jnp.einsum('ech,ehd->ecd', h1, w2) + b2[:, None, :]
            out_buf = h2.reshape(E * CAP, D)
            y_s = jnp.where(valid[:, None], out_buf[jnp.minimum(slot, E * CAP - 1)], 0.0)
            return jnp.zeros((N, D), x.dtype).at[tok_s].add(g_s[:, None] * y_s)

        def _forward(feats, W_gc, b_gc, W_res, b_res, Wg, bg, w1, b1, w2, b2, gamma, beta, src, dst):
            n = feats.shape[0]
            ones = jnp.ones((src.shape[0],), feats.dtype)
            deg_out = jnp.clip(jax.ops.segment_sum(ones, src, num_segments=n), 1.0)
            deg_in = jnp.clip(jax.ops.segment_sum(ones, dst, num_segments=n), 1.0)
            h = feats * jax.lax.rsqrt(deg_out)[:, None]
            m = jax.ops.segment_sum(h[src], dst, num_segments=n) * jax.lax.rsqrt(deg_in)[:, None]
            gc = m @ W_gc + b_gc
            x = gc + (feats @ W_res + b_res)
            core = _moe_ff(x, Wg, bg, w1, b1, w2, b2)
            y = x + core
            mean = jnp.mean(y, axis=0)
            var = jnp.mean((y - mean) ** 2, axis=0)
            return (y - mean) * jax.lax.rsqrt(var + BN_EPS) * gamma + beta
        return _forward(feats, W_gc, b_gc, W_res, b_res, Wg, bg, w1, b1, w2, b2, gamma, beta, src, dst)
    x = _layernorm(x + _L0_gnn_ref(x, L0_gnn_W_gc, L0_gnn_b_gc, L0_gnn_W_res, L0_gnn_b_res, L0_gnn_Wg, L0_gnn_bg, L0_gnn_w1, L0_gnn_b1, L0_gnn_w2, L0_gnn_b2, L0_gnn_gamma, L0_gnn_beta, src, dst), axis=-1)
    return x

_drawn_inputs = setup_inputs


def setup_inputs(seed=0):
    import zlib

    import numpy as np

    out = dict(_drawn_inputs(seed))
    spreads = {'L0_gnn_b_gc': (0.0, 0.1),
     'L0_gnn_b_res': (0.0, 0.1),
     'L0_gnn_bg': (0.0, 0.1),
     'L0_gnn_b1': (0.0, 0.1),
     'L0_gnn_b2': (0.0, 0.1),
     'L0_gnn_gamma': (1.0, 0.2),
     'L0_gnn_beta': (0.0, 0.1)}
    factors = {}
    for name, (base, spread) in spreads.items():
        noise = np.random.default_rng([zlib.crc32(name.encode()), seed]).standard_normal(out[name].shape)
        drawn = base * np.exp(spread * noise) if base else spread * noise
        out[name] = jnp.asarray(drawn.astype(out[name].dtype))
    for name, factor in factors.items():
        out[name] = (out[name] * factor).astype(out[name].dtype)
    return out
```

```python
from contextlib import ExitStack

import concourse.bass as bass
from concourse import mybir

ALU = mybir.AluOpType
ACT = mybir.ActivationFunctionType
AX = mybir.AxisListType
F32 = mybir.dt.float32
F32R = mybir.dt.float32r
BF16 = mybir.dt.bfloat16
I32 = mybir.dt.int32
U32 = mybir.dt.uint32
ds = bass.ds

P = 128
CAP = 1024
EPS = 1e-5
RING = 8
AHEAD = 6
HC = 16
ROW = 256
WN = 2
WB = 8
OHB = 4
NOWHERE = 1 << 20
SC = 8


def gnn_kernel(nc, x, src, dst, W_gc, b_gc, W_res, b_res, Wg, bg, w1, b1, w2, b2, gamma, beta, out):
    N, D = x.shape
    E = src.shape[0]
    NEXP = Wg.shape[1]
    H = w1.shape[2]
    K, HK = D // P, H // P
    NB = -(-N // P)
    NPAD = NB * P
    TAIL = N - (NB - 1) * P
    EC = E // P
    EREST = E - EC * P
    NHG = -(-(EC + 1) // HC)
    LEAD = 5
    NROW = -(-E // ROW)
    PADROWS = -(-(NROW * ROW + P) // (P * SC)) * (P * SC) // ROW
    EPAD = PADROWS * ROW
    NSG = EPAD // (P * SC)
    NWT = -(-(NB * P // WN) // P)
    WPB = P // WN
    BPB = WPB // WB
    WV = WN * NB
    LROWS = CAP + P
    NSLOT = NEXP * LROWS
    TMAX = (2 * N + NEXP * (P - 1)) // P + 1
    TLOOP = -(-(TMAX + 1) // RING) * RING
    CE, CJ = RING.bit_length() - 1, (RING * NEXP).bit_length() - 1
    NPAIR = (NB - 1) // 2
    BPG = 8
    NFG = (NB - 1) // BPG
    BLK7 = 7
    NPC = NB // BLK7
    assert NB % BLK7 == 0 and (NB - 1) % (2 * BPG) == 0 and NPAIR * 2 + 1 == NB and NPAIR % 2 == 0
    assert NHG % 2 == 1 and NROW % 2 == 0 and BPB == 2 * OHB and NB % 2 == 1 and NHG // 2 - LEAD < NB and WV * 4 <= 512

    restab = nc.dram_tensor("restab", (NPAD, D), F32, kind="Internal").ap()
    xtab = nc.dram_tensor("xtab", (NPAD, D), F32, kind="Internal").ap()
    htab = nc.dram_tensor("htab", (NPAD, D), F32, kind="Internal").ap()
    srcpad = nc.dram_tensor("srcpad", (PADROWS, ROW), I32, kind="Internal").ap()
    dstpad = nc.dram_tensor("dstpad", (PADROWS, ROW), I32, kind="Internal").ap()
    lists = nc.dram_tensor("lists", (NSLOT, 4), I32, kind="Internal").ap()
    ytab = nc.dram_tensor("ytab", (2 * N + P, D), F32, kind="Internal").ap()
    src_flat = srcpad.rearrange("r c -> (r c)")
    dst_flat = dstpad.rearrange("r c -> (r c)")

    with ExitStack() as ctx:
        def sb(name, shape, dt=F32):
            return ctx.enter_context(nc.sbuf_tensor(name, shape, dt))

        def sem(name):
            return ctx.enter_context(nc.semaphore(name))

        with nc.sbuf_tensor("parts_r", [P, NB * 2 * D], F32R) as parts_r:
            parts = parts_r[:, :].rearrange("p (b d) -> p b d", b=NB)
        big = sb("big", [P, NB * 2 * D])
        G = big[:, :].rearrange("p (b d) -> p b d", b=NB)
        F = big[:, 0:NB * D].rearrange("p (b d) -> p b d", b=NB)
        FB = NB * D
        ybuf = big[:, FB:FB + 2 * BPG * 2 * D].rearrange("p (s b k d) -> p s b k d", s=2, b=BPG, k=2)
        sqbuf = big[:, FB:FB + 2 * BPG * D].rearrange("p (s b d) -> p s b d", s=2, b=BPG)
        fbuf = big[:, FB + 2 * BPG * 2 * D:FB + 3 * BPG * 2 * D].rearrange("p (s b d) -> p s b d", s=2, b=BPG)

        AW = 2 * NB * P
        OHW = OHB * WB * (P + WV) // 2
        with nc.sbuf_tensor("counts_r", [P, AW], F32R) as counts_r:
            counts = [counts_r[:, h * NB * P:(h + 1) * NB * P].rearrange("p (b n) -> p b n", b=NB) for h in range(2)]
        work = sb("work", [P, AW + OHW])

        def part(at, words):
            return work[:, at:at + words]
        OH1, OH2 = WB * P // 2, WB * WV // 2
        oh_lo = [part(AW + s * OH1, OH1).bitcast(BF16).rearrange("p (v w) -> p v w", w=WB) for s in range(OHB)]
        oh_v = [part(AW + OHB * OH1 + s * OH2, OH2).bitcast(BF16).rearrange("p (v w) -> p v w", w=WB) for s in range(OHB)]
        HB1, HB2 = HC * P // 2, HC * NB // 2
        hist_lo = [part(AW + s * HB1, HB1).bitcast(BF16).rearrange("p (v c) -> p v c", c=HC) for s in range(2)]
        hist_hi = [part(AW + 2 * HB1 + s * HB2, HB2).bitcast(BF16).rearrange("p (v c) -> p v c", c=HC) for s in range(2)]
        EW = NHG * HC
        src_i = part(0, EW).bitcast(I32)
        digit_i = part(EW, EW).bitcast(I32)
        iota_lo16 = part(2 * EW, HB1).bitcast(BF16).rearrange("p (v c) -> p v c", c=HC)
        iota_hi16 = part(2 * EW + HB1, HB2).bitcast(BF16).rearrange("p (v c) -> p v c", c=HC)
        A1 = 2 * EW + HB1 + HB2
        bases_i = work[0:1, A1:A1 + NROW].bitcast(I32)
        bases_f = work[0:1, A1:A1 + NROW]
        spare = part(A1 + NROW, NROW // 2).bitcast(BF16)
        pick = part(A1, 4 * P).rearrange("p (m n) -> p m n", m=4)
        A2 = AW - NWT * ROW
        found = part(A2, NWT * ROW).bitcast(I32).rearrange("p (t c) -> p t c", t=NWT)
        dst_w = part(A2, NWT * P).bitcast(I32).rearrange("p (t c) -> p t c", t=NWT)
        src_w = part(A2 + NWT * P, NWT * P).bitcast(I32).rearrange("p (t c) -> p t c", t=NWT)
        rel_w = part(A2, NWT * P).rearrange("p (t c) -> p t c", t=NWT)
        low_w = part(A2 + NWT * P, NWT * P).rearrange("p (t c) -> p t c", t=NWT)
        hi_w = part(0, NWT * P).bitcast(I32).rearrange("p (t c) -> p t c", t=NWT)
        padlist = part(A2, NSLOT // P * 4).bitcast(I32).rearrange("p (r c) -> p r c", c=4)
        A3 = A2 + NSLOT // P * 4
        PADS = EPAD - E
        padends = work[0:1, A3:A3 + 2 * PADS].bitcast(I32).rearrange("p (m c) -> p m c", m=2)
        assert A1 + NROW + NROW // 2 <= A2 and A3 + 2 * PADS <= AW and 2 * (HB1 + HB2) <= OHW and NWT * P <= A2
        piece = [part(s * BLK7 * D, BLK7 * D).rearrange("p (b d) -> p b d", b=BLK7) for s in range(2)]
        slow_sums = part(0, NB * D).rearrange("p (b d) -> p b d", b=NB)
        slow_rows = part(AW, SC * D).rearrange("p (c d) -> p c d", c=SC)
        slow_hot = part(AW + SC * D, SC * P).rearrange("p (c n) -> p c n", c=SC)
        assert SC * (D + P) <= OHW and 2 * BLK7 <= NB
        w1s = part(0, RING * K * H).rearrange("p (s k h) -> p s k h", s=RING, k=K)
        w2s = big[:, FB:FB + RING * HK * D].rearrange("p (s k d) -> p s k d", s=RING, k=HK)
        b2s = big[:, FB + RING * HK * D:FB + RING * (HK + 1) * D].rearrange("p (s d) -> p s d", s=RING)
        T0 = RING * K * H
        xg = part(T0, RING * D).rearrange("p (s d) -> p s d", s=RING)
        T1 = T0 + RING * D
        xT = part(T1, 2 * D).rearrange("p (s k n) -> p s k n", s=2, k=K)
        T2 = T1 + 2 * D
        h1 = part(T2, 2 * H).rearrange("p (s k n) -> p s k n", s=2, k=HK)
        T3 = T2 + 2 * H
        hs = part(T3, 2 * H).rearrange("p (s h) -> p s h", s=2)
        T4 = T3 + 2 * H
        yo = part(T4, RING * D).rearrange("p (s d) -> p s d", s=RING)
        T5 = T4 + RING * D
        b1_s = work[0:NEXP, T5:T5 + H]
        assert T5 + H <= AW + OHW and T5 >= AW and FB + RING * (HK + 1) * D <= NB * 2 * D

        NWIN = NWT * P
        edge = sb("edge", [P, NWIN])
        edge_lo = edge[:, 0:NWIN // 2].bitcast(BF16)
        edge_v = edge[:, NWIN // 2:NWIN].bitcast(BF16)
        src_lo = edge[:, 0:EW // 2].bitcast(BF16).rearrange("p (g c) -> p g c", g=NHG)
        src_hi = edge[:, NWIN // 2:NWIN // 2 + EW // 2].bitcast(BF16).rearrange("p (g c) -> p g c", g=NHG)
        ended = edge[0:NEXP, 0:192]
        tile_f = edge[0:1, 192:192 + 4 * 192].rearrange("p (r t) -> p r t", r=4)
        tile_i = edge[0:1, 960:960 + 2 * 192].bitcast(I32).rearrange("p (r t) -> p r t", r=2)

        iota_lo = sb("iota_lo", [P, P, WB], BF16)
        iota_v = sb("iota_v", [P, WV, WB], BF16)
        iota_i = sb("iota_i", [P, 128], I32)
        pcol_i = sb("pcol_i", [P, 1], I32)
        win_i = sb("win_i", [P, NWT], I32)
        iota = sb("iota", [P, 192])
        pcol = sb("pcol", [P, 1])
        pcols = sb("pcols", [P, 4])
        ident = sb("ident", [P, P])
        onesf = sb("onesf", [P, P])
        zeros = sb("zeros", [P, D])
        tri_b = sb("tri_b", [P, P], BF16)
        tri_eq = sb("tri_eq", [P, P])
        ones_b = sb("ones_b", [P, P], BF16)
        first_w = sb("first_w", [P, NWT])
        below = sb("below", [P, 3, NWT])
        signs = sb("signs", [P, 5, NWT])
        row_w = sb("row_w", [P, NWT], I32)
        edge_w = sb("edge_w", [P, NWT], I32)
        deg_w = sb("deg_w", [P, WN, NWT])
        held = sb("held", [P, 1])
        general_f = sb("general_f", [1, 1])
        general = sb("general", [1, 1], I32)

        Wg_s = sb("Wg_s", [P, K, NEXP])
        bg_s = sb("bg_s", [P, NEXP])
        gb_s = sb("gb_s", [P, 2, D])
        b1T = sb("b1T", [P, HK, NEXP])

        degs = sb("degs", [P, 2, NB])
        rs_out = sb("rs_out", [P, NB])
        rs_in = sb("rs_in", [P, 2 * NWT])
        pair_mem = sb("pair_mem", [P, 4 * D])
        pair_x = [pair_mem[:, s * 2 * D:(s + 1) * 2 * D].rearrange("p (b d) -> p b d", b=2) for s in range(2)]
        fblk = pair_mem[:, 0:D]
        bias_x = pair_mem[:, 2 * D:4 * D].rearrange("p (m d) -> p m d", m=2)
        mean, scale = pair_mem[:, 0:D], pair_mem[:, D:2 * D]
        res_mem = sb("res_mem", [P, 4 * D])
        res_buf = [res_mem[:, s * 2 * D:(s + 1) * 2 * D].rearrange("p (b d) -> p b d", b=2) for s in range(2)]
        Wx_s = res_mem[:, :].rearrange("p (k m d) -> p k m d", k=K, m=2)
        xTp = sb("xTp", [P, 2, K, P])
        fT = [xTp[:, s] for s in range(2)]
        picks = sb("picks", [P, 2, 2, 2, NEXP])
        ranked = sb("ranked", [P, 2, 2, NEXP])

        logit = sb("logit", [P, 2, NEXP])
        top8 = sb("top8", [P, 2, 8])
        top8i = sb("top8i", [P, 2, 8], U32)
        expert = sb("expert", [P, 2, 2, 2])
        both = sb("both", [P, 2, 2, NEXP], BF16)
        before = sb("before", [P, 2, NEXP], BF16)
        gap = sb("gap", [P, 2, 2])
        egap = sb("egap", [P, 2, 2])
        rank = sb("rank", [P, 2, 2])
        over = sb("over", [P, 2, 2])
        slot_f = sb("slot_f", [P, 2, 2])
        slot = sb("slot", [P, 2, 2, 2], I32)
        entry = sb("entry", [P, 2, 2, 2, 4], I32)
        tok_i = sb("tok_i", [P, NB, 2, 2], I32)

        cntc = sb("cntc", [NEXP, 8])
        cnti = sb("cnti", [NEXP, 2], I32)
        last_i = sb("last_i", [1, 1], I32)

        lt = sb("lt", [P, RING, 4], I32)

        slow_src = sb("slow_src", [P, SC], I32)
        slow_dst = sb("slow_dst", [P, SC], I32)
        slow_rel = sb("slow_rel", [P, SC])

        stats = sb("stats", [P, BPG, 6])
        moments = sb("moments", [P, BPG, 2])
        inv = sb("inv", [P, BPG])
        eps_c = sb("eps_c", [P, 1])

        banks = ctx.enter_context(nc.psum_tensor("banks", [P, 8, 512], F32))
        bank = [banks[:, i, :] for i in range(8)]
        hist_ps = bank[0][:, 0:NB]
        prod_ps = [bank[1], bank[2]]
        fT_ps = bank[3][:, 0:K * P].rearrange("p (k n) -> p k n", k=K)
        bases_ps = banks[:, 4:6, 0:NROW // 2]
        small = bank[4]
        turned_ps = [bank[6 + m].rearrange("p (t n) -> p t n", t=4) for m in range(2)]
        built_ps = [banks[:, 2 * s:2 * s + 2, :] for s in range(2)]
        agg_ps = [bank[4], bank[5]]
        slow_ps = bank[5]
        xT_ps = bank[6].rearrange("p (b k n) -> p b k n", b=2, k=K)
        logit_ps = bank[7][:, 0:2 * NEXP].rearrange("p (b e) -> p b e", b=2)
        rank_ps = bank[7][:, 2 * NEXP:4 * NEXP].rearrange("p (b e) -> p b e", b=2)
        tx_ps = [bank[i][:, 0:K * P].rearrange("p (k n) -> p k n", k=K) for i in (0, 1)]
        h_ps = [bank[i] for i in (2, 3)]
        hT_ps = [bank[i].rearrange("p (k n) -> p k n", k=HK) for i in (6, 7)]
        y_ps = [bank[i][:, 0:D] for i in (4, 5)]
        sum_ps, sq_ps = bank[6][:, 0:D], bank[7][:, 0:D]

        src_in, feats_in, weights_in, bases_in, pads_out = sem("src_in"), sem("feats_in"), sem("weights_in"), sem("bases_in"), sem("pads_out")
        tails_set, lists_set, lists_out, y_zeroed = sem("tails_set"), sem("lists_set"), sem("lists_out"), sem("y_zeroed")
        iotas, consts, b1_in = sem("iotas"), sem("consts"), sem("b1_in")
        hist_ready, hist_used, hist_done = sem("hist_ready"), sem("hist_used"), sem("hist_done")
        deg_clipped, deg_root, rs_ready = sem("deg_clipped"), sem("deg_root"), sem("rs_ready")
        f_staged, fT_summed, fT_ready = sem("f_staged"), sem("fT_summed"), sem("fT_ready")
        bias_ready, multiplied, prod_copied = sem("bias_ready"), sem("multiplied"), sem("prod_copied")
        res_out = [sem(f"res_out{j}") for j in range(NPC)]
        upper_ready, split = sem("upper_ready"), sem("split")
        bases_float, bases_ready, rows_counted, row_ready = sem("bases_float"), sem("bases_ready"), sem("rows_counted"), sem("row_ready")
        found_in, found_counted, edge_ready = sem("found_in"), sem("found_counted"), sem("edge_ready")
        dst_w_in, src_w_in, window_counted = sem("dst_w_in"), sem("src_w_in"), sem("window_counted")
        digits_ready, digits_turned, edges_ready = sem("digits_ready"), sem("digits_turned"), sem("edges_ready")
        deg_ready, deg_placed, general_ready, blocks_ready = sem("deg_ready"), sem("deg_placed"), sem("general_ready"), sem("blocks_ready")
        piece_ready, piece_out = sem("piece_ready"), [sem("piece_out0"), sem("piece_out1")]
        slow_edges_in, slow_rows_in, slow_hot_ready, slow_summed, slow_used = (
            sem("slow_edges_in"), sem("slow_rows_in"), sem("slow_hot_ready"), sem("slow_summed"), sem("slow_used"))
        slow_res_in, slow_added, slow_res_out = sem("slow_res_in"), sem("slow_added"), sem("slow_res_out")
        onehot_ready, built, evacuated, summed, x_made, res_in = (
            sem("onehot_ready"), sem("built"), sem("evacuated"), sem("summed"), sem("x_made"), [sem("res_in0"), sem("res_in1")])
        x_turned, xT_ready = sem("x_turned"), sem("xT_ready")
        logits_done, both_ready, gap_ready, egap_ready = sem("logits_done"), sem("both_ready"), sem("gap_ready"), sem("egap_ready")
        ranks_done, slots_ready = sem("ranks_done"), sem("slots_ready")
        list_out = [sem("list_out0"), sem("list_out1")]
        x_out = [sem("x_out0"), sem("x_out1")]
        x_in = sem("x_in")
        tables, tables_col, tiles_ready, b1_turned, b1_ready = (
            sem("tables"), sem("tables_col"), sem("tiles_ready"), sem("b1_turned"), sem("b1_ready"))
        list_in = [sem(f"list_in{s}") for s in range(RING)]
        y_out = [sem(f"y_out{s}") for s in range(RING)]
        xg_in = [sem(f"xg_in{s}") for s in range(RING)]
        w_in = [sem(f"w_in{s}") for s in range(RING)]
        tx_done, tx_ready, h_done, hs_ready, hT_done, h1_ready, tile_done, y_ready = (
            sem("tx_done"), sem("tx_ready"), sem("h_done"), sem("hs_ready"), sem("hT_done"), sem("h1_ready"), sem("tile_done"), sem("y_ready"))
        y_in = [sem("y_in0"), sem("y_in1")]
        y_summed, sum_done = sem("y_summed"), sem("sum_done")
        centred, squared, sq_done, sq_used = sem("centred"), sem("squared"), sem("sq_done"), sem("sq_used")
        root_ready, var_ready, f_in, f_ready, f_used = (
            sem("root_ready"), sem("var_ready"), [sem("f_in0"), sem("f_in1")], sem("f_ready"), sem("f_used"))
        lnvar_ready, lnroot_ready, out_ready, out_done = sem("lnvar_ready"), sem("lnroot_ready"), sem("out_ready"), sem("out_done")

        block = ctx.enter_context(nc.Block())

        def x_out_total(parity):
            return 16 * sum(j % 2 == parity for j in range(NPAIR + 1))

        def list_out_total(parity):
            return sum(2 * (2 if j < NPAIR else 1) for j in range(NPAIR + 1) if j % 2 == parity)

        def blocks(a, b0, n):
            return a[b0 * P:(b0 + n) * P, :].rearrange("(b p) d -> p b d", p=P)

        def blocks_of(j):
            return 1 if isinstance(j, int) and j == NPAIR else 2

        def rows_of(j):
            return TAIL if isinstance(j, int) and j == NPAIR else P

        def fifth(q):
            return range(-(-q * NB // 5), -(-(q + 1) * NB // 5))

        NW = 16 * 8
        B_FOUND, B_WINDOW = (10, 6), (26, 12)
        G_ROW, G_EDGE, G_DIGITS = 6, 21, 46

        @block.sync
        def _(sp):
            sp.dma_start(src_i[:, 0:EC], src[0:EC * P].rearrange("(p c) -> p c", p=P)).then_inc(src_in, 16)
            sp.dma_start(bases_i[:, 0:NROW - 1], dst[0:(NROW - 1) * ROW].rearrange("(r c) -> r c", c=ROW)[:, 0:1].rearrange("r c -> c r"),
                         allow_slow_non_contiguous=True).then_inc(bases_in, 16)
            sp.dma_start(bases_i[:, NROW - 1:NROW], dst[(NROW - 1) * ROW:(NROW - 1) * ROW + 1].rearrange("(p c) -> p c", p=1)).then_inc(bases_in, 16)
            sp.wait_ge(tails_set, 1)
            sp.dma_start(src_i[0:EREST, EC:EC + 1], src[EC * P:E].rearrange("(p c) -> p c", c=1)).then_inc(src_in, 16)
            for m, (a, flat) in enumerate(((dst, dst_flat), (src, src_flat))):
                sp.dma_start(flat[0:EC * P].rearrange("(p c) -> p c", p=P), a[0:EC * P].rearrange("(p c) -> p c", p=P)).then_inc(pads_out, 16)
                sp.dma_start(flat[EC * P:E].rearrange("(p c) -> p c", p=1), a[EC * P:E].rearrange("(p c) -> p c", p=1)).then_inc(pads_out, 16)
                sp.dma_start(flat[E:EPAD].rearrange("(p c) -> p c", p=1), padends[:, m, :]).then_inc(pads_out, 16)
            sp.dma_start(G[:, 0:2 * BLK7, D:2 * D], blocks(x, 0, 2 * BLK7)).then_inc(feats_in, 16)
            sp.dma_start(G[:, 2 * BLK7:NB - 1, D:2 * D], blocks(x, 2 * BLK7, NB - 1 - 2 * BLK7)).then_inc(feats_in, 16)
            sp.dma_start(G[0:TAIL, NB - 1, D:2 * D], x[(NB - 1) * P:N, :]).then_inc(feats_in, 16)
            sp.wait_ge(lists_set, 1)
            sp.dma_start(lists.rearrange("(p r) c -> p (r c)", p=P), padlist[:, :, :].rearrange("p r c -> p (r c)")).then_inc(lists_out, 16)
            for j in range(NPC):
                sp.wait_ge(prod_copied, (j + 1) * BLK7 + 2)
                sp.dma_start(blocks(restab, j * BLK7, BLK7), G[:, j * BLK7:(j + 1) * BLK7, D:2 * D]).then_inc(res_out[j], 16)
            for j in range(NPC):
                sp.wait_ge(res_out[j], 16)
            sp.wait_ge(consts, 1)
            n = N * 2 // P
            sp.dma_start(ytab[0:n * P, :].rearrange("(p r) d -> p r d", p=P),
                         zeros[:, :].unsqueeze(1).to_broadcast([P, n, D])).then_inc(y_zeroed, 16)
            sp.dma_start(ytab[n * P:2 * N, :], zeros[0:2 * N - n * P, :]).then_inc(y_zeroed, 16)
            sp.wait_ge(general_ready, 1)
            is_general = sp.value_load(general[0:1, 0:1], min_val=0, max_val=1)
            with sp.If(is_general > 0):
                for j in range(NPC):
                    sp.wait_ge(piece_ready, j + 1)
                    sp.dma_start(blocks(htab, j * BLK7, BLK7), piece[j % 2]).then_inc(piece_out[j % 2], 16)
                with sp.Fori(0, NSG) as g:
                    sp.wait_ge(slow_used, g + 1)
                    sp.dma_start(slow_src[:, :], src_flat[ds(g * (P * SC), P * SC)].rearrange("(p c) -> p c", p=P)).then_inc(slow_edges_in, 16)
                    sp.dma_start(slow_dst[:, :], dst_flat[ds(g * (P * SC), P * SC)].rearrange("(p c) -> p c", p=P)).then_inc(slow_edges_in, 16)
                with sp.Fori(0, NB) as b:
                    sp.dma_start(fblk, restab[ds(b * P, P), :]).then_inc(slow_res_in, 16)
                    sp.wait_ge(slow_added, b + 1)
                    sp.dma_start(restab[ds(b * P, P), :], fblk).then_inc(slow_res_out, 16)
                    stored = sp.to_reg(b * 16 + 16)
                    sp.wait_ge(general_ready, 1)
                    sp.wait_ge(slow_res_out, stored)

            def load_res(j, s, nb):
                sp.dma_start(res_buf[s][:, 0:nb, :], restab[ds(j * (2 * P), nb * P), :].rearrange("(b p) d -> p b d", p=P)).then_inc(res_in[s], 16)

            def store_x(j, s, nb):
                sp.wait_ge(x_made, j * 2 + (nb + 2))
                sp.dma_start(xtab[ds(j * (2 * P), nb * P), :].rearrange("(b p) d -> p b d", p=P), pair_x[s][:, 0:nb, :]).then_inc(x_out[s], 16)

            sp.wait_ge(prod_copied, NB + 2)
            for s in range(2):
                load_res(s, s, 2)
            with sp.Fori(0, NPAIR // 2 - 1) as i:
                for s in range(2):
                    store_x(i * 2 + s, s, 2)
                    load_res(i * 2 + (s + 2), s, 2)
            store_x(NPAIR - 2, 0, 2)
            load_res(NPAIR, 0, 1)
            store_x(NPAIR - 1, 1, 2)
            store_x(NPAIR, 0, 1)
            for s in range(2):
                sp.wait_ge(x_out[s], x_out_total(s))
            sp.dma_start(F[:, :, :], blocks(xtab, 0, NB)).then_inc(x_in, 16)
            sp.wait_ge(tiles_ready, 1)
            for s in range(2):
                sp.wait_ge(list_out[s], 16 * list_out_total(s))
            last = sp.value_load(last_i[0:1, 0:1], min_val=1, max_val=TMAX)
            with sp.Fori(0, TLOOP // RING) as i:
                for s in range(RING):
                    t = i * RING + s
                    with sp.If(t < last + 1):
                        code = sp.value_load(tile_i[0:1, 0, ds(t, 1)], min_val=0, max_val=(8 * NEXP * RING) - 1)
                        e = sp.snap((code >> CE) & (NEXP - 1))
                        j = sp.snap((code >> CJ) & (CAP // P - 1))
                        ws = sp.snap(code & (RING - 1))
                        sent, used, at = sp.to_reg(i * 16 + 16), sp.to_reg(t + 1), sp.snap(e * LROWS + j * P)
                        sp.wait_ge(tiles_ready, 1)
                        sp.wait_ge(y_out[s], sent)
                        sp.wait_ge(tile_done, used)
                        sp.dma_start(lt[:, s, :], lists[ds(at, P), :]).then_inc(list_in[s], 16)
                        with sp.If(j == 0):
                            sp.dma_start(w1s[:, ds(ws, 1), :, :].rearrange("p s k h -> p (s k) h"),
                                         w1[ds(e, 1), :, :].rearrange("e (k p) h -> p (e k) h", p=P)).then_inc(w_in[s], 16)
                            sp.dma_start(w2s[:, ds(ws, 1), :, :].rearrange("p s k d -> p (s k) d"),
                                         w2[ds(e, 1), :, :].rearrange("e (k p) d -> p (e k) d", p=P)).then_inc(w_in[s], 16)
                            sp.dma_start(b2s[:, ds(ws, 1), :].rearrange("p s d -> p (s d)"),
                                         b2[ds(e, 1), :].to_broadcast([P, D])).then_inc(w_in[s], 16)
                        with sp.Else():
                            sp.sem_inc(w_in[s], 48)
            n_tiles = sp.snap(last)
            for s in range(RING):
                sent = sp.to_reg(((n_tiles + (RING - 1 - s)) // RING) * 16 + 16)
                sp.wait_ge(tiles_ready, 1)
                sp.wait_ge(y_out[s], sent)
            yv = ytab[0:2 * (NB - 1) * P, :].rearrange("(g b p k) d -> g p b (k d)", b=BPG, p=P, k=2)
            with sp.Fori(0, NFG // 2) as i:
                for s in range(2):
                    sp.wait_ge(y_summed, i * 2 + (s + 1))
                    sp.dma_start(ybuf[:, s].rearrange("p b k d -> p b (k d)"),
                                 yv[ds(i * 2 + s, 1)].rearrange("g p b e -> p (g b) e")).then_inc(y_in[s], 16)
            sp.wait_ge(y_summed, NFG + 1)
            sp.dma_start(ybuf[0:TAIL, 0, 0].rearrange("p k d -> p (k d)"),
                         ytab[2 * (NB - 1) * P:2 * N, :].rearrange("(p k) d -> p (k d)", k=2)).then_inc(y_in[0], 16)
            xv = x[0:(NB - 1) * P, :].rearrange("(g b p) d -> g p b d", b=BPG, p=P)
            ov = out[0:(NB - 1) * P, :].rearrange("(g b p) d -> g p b d", b=BPG, p=P)
            for g in range(2):
                sp.dma_start(fbuf[:, g], xv[g]).then_inc(f_in[g], 16)
            for g in range(NFG):
                sp.wait_ge(out_ready, g + 1)
                sp.dma_start(ov[g], F[:, g * BPG:(g + 1) * BPG, :]).then_inc(out_done, 16)
                if g + 2 < NFG:
                    sp.wait_ge(f_used, g + 1)
                    sp.dma_start(fbuf[:, g % 2], xv[g + 2]).then_inc(f_in[g % 2], 16)
                elif g + 2 == NFG:
                    sp.wait_ge(f_used, g + 1)
                    sp.dma_start(fbuf[0:TAIL, g % 2, 0], x[(NB - 1) * P:N, :]).then_inc(f_in[g % 2], 16)
            sp.wait_ge(out_ready, NFG + 1)
            sp.dma_start(out[(NB - 1) * P:N, :], F[0:TAIL, NB - 1, :]).then_inc(out_done, 16)
            sp.wait_ge(out_done, 16 * (NFG + 1))

        @block.gpsimd
        def _(pool):
            pool.iota(iota_i[:, :], [[1, 128]], base=0, channel_multiplier=0)
            pool.iota(win_i[:, :], [[WN * P, NWT]], base=0, channel_multiplier=WN)
            pool.iota(pcol_i[:, :], [[0, 1]], base=0, channel_multiplier=1).then_inc(iotas, 1)
            pool.iota(tok_i[:, :, :, 0], [[P, NB], [0, 2]], base=0, channel_multiplier=1)
            pool.iota(tok_i[:, :, :, 1], [[2 * P, NB], [1, 2]], base=0, channel_multiplier=2).then_inc(iotas, 1)
            pool.wait_ge(pads_out, 16 * 6)
            pool.wait_ge(lists_out, 16)
            pool.wait_ge(row_ready, 1)
            for t in range(NWT):
                pool.indirect_dma_start(found[:, t, :], None, dstpad, bass.IndirectOffsetOnAxis(ap=row_w[:, t:t + 1], axis=0)).then_inc(found_in, 16)
            pool.wait_ge(edge_ready, 1)
            for ends, flat, done in ((dst_w, dst_flat, dst_w_in), (src_w, src_flat, src_w_in)):
                for t in range(NWT):
                    pool.indirect_dma_start(ends[:, t, :], None, flat.rearrange("(n o) -> n o", o=1),
                                            bass.IndirectOffsetOnAxis(ap=edge_w[:, t:t + 1], axis=0)).then_inc(done, 16)

            pool.wait_ge(general_ready, 1)
            is_general = pool.value_load(general[0:1, 0:1], min_val=0, max_val=1)
            with pool.If(is_general > 0):
                for s in range(2):
                    pool.wait_ge(piece_out[s], 16 * sum(j % 2 == s for j in range(NPC)))
                with pool.Fori(0, NSG) as g:
                    loaded = pool.to_reg(g * 32 + 32)
                    pool.wait_ge(general_ready, 1)
                    pool.wait_ge(slow_edges_in, loaded)
                    for c in range(SC):
                        pool.indirect_dma_start(slow_rows[:, c, :], None, htab, bass.IndirectOffsetOnAxis(ap=slow_src[:, c:c + 1], axis=0)
                                                ).then_inc(slow_rows_in, 16)

            pool.wait_ge(y_zeroed, 32)
            for s in range(RING):
                pool.dma_start(ytab[2 * N + s:2 * N + s + 1, :], zeros[0:1, :]).then_inc(y_out[s], 16)

            def send(j, s, nb, valid):
                placed = pool.to_reg(j + 1)
                pool.wait_ge(lists_out, 16)
                pool.wait_ge(slots_ready, placed)
                for b in range(nb):
                    for k in range(2):
                        pool.indirect_dma_start(lists, bass.IndirectOffsetOnAxis(ap=slot[0:valid, s, b, k:k + 1], axis=0),
                                                entry[0:valid, s, b, k, :], None, bounds_check=NSLOT - 1, oob_is_err=False
                                                ).then_inc(list_out[s], 16)

            with pool.Fori(0, NPAIR // 2) as i:
                for s in range(2):
                    send(i * 2 + s, s, 2, P)
            send(NPAIR, NPAIR % 2, 1, TAIL)

            for s in range(2):
                pool.wait_ge(x_out[s], x_out_total(s))
            pool.wait_ge(tiles_ready, 1)
            last = pool.value_load(last_i[0:1, 0:1], min_val=1, max_val=TMAX)

            def fetch(t, i, s):
                with pool.If(t < last + 1):
                    listed, turned = pool.to_reg(i * 16 + 16), pool.to_reg(t + 1)
                    pool.wait_ge(tiles_ready, 1)
                    pool.wait_ge(list_in[s % RING], listed)
                    pool.wait_ge(tx_done, turned)
                    pool.indirect_dma_start(xg[:, s % RING, :], None, xtab, bass.IndirectOffsetOnAxis(ap=lt[:, s % RING, 0:1], axis=0)
                                            ).then_inc(xg_in[s % RING], 16)

            for t in range(AHEAD):
                fetch(t, 0, t)
            with pool.Fori(0, TLOOP // RING) as i:
                for s in range(RING):
                    t = i * RING + s
                    with pool.If(t < last):
                        done = pool.to_reg(t + 3)
                        pool.wait_ge(tiles_ready, 1)
                        pool.wait_ge(y_ready, done)
                        pool.indirect_dma_start(ytab, bass.IndirectOffsetOnAxis(ap=lt[:, s, 1:2], axis=0), yo[:, s, :], None,
                                                bounds_check=2 * N - 1, oob_is_err=False
                                                ).then_inc(y_out[s], 16)
                    fetch(t + AHEAD, i + (s + AHEAD) // RING, s + AHEAD)

            for g in range(NFG + 1):
                pool.wait_ge(f_in[g % 2], 16 * (g // 2 + 1))
                v, n = (fbuf[:, g % 2], BPG) if g < NFG else (fbuf[0:TAIL, g % 2, 0:1], 1)
                q = P if g < NFG else TAIL
                pool.tensor_tensor(v, v, gb_s[0:q, 1, :].unsqueeze(1).to_broadcast([q, n, D]), ALU.add).then_inc(f_ready, 1)

        @block.scalar
        def _(act):
            for m, w in enumerate((W_gc, W_res)):
                act.dma_start(Wx_s[:, :, m, :], w.rearrange("(k p) n -> p k n", p=P)).then_inc(weights_in, 16)
            act.dma_start(Wg_s[:, :, :], Wg.rearrange("(k p) n -> p k n", p=P)).then_inc(weights_in, 16)
            for tile, v in ((bias_x[:, 0, :], b_gc), (bias_x[:, 1, :], b_res), (bg_s[:, :], bg),
                            (gb_s[:, 0, :], gamma), (gb_s[:, 1, :], beta)):
                act.dma_start(tile, v.unsqueeze(0).to_broadcast([P, v.shape[0]])).then_inc(weights_in, 16)

            def count_below(signs_out, ends, threshold, total):
                nc.scalar.activation(signs_out, ends, ACT.Sign, bias=threshold, scale=-1.0, accum_out=total)

            nc.scalar.preload_act_table(ACT.Sign)

            def stage_feats(b):
                if not isinstance(b, int) or b > 0:
                    act.wait_ge(fT_summed, b)
                nc.scalar.copy(fblk, G[:, ds(b, 1), D:2 * D].rearrange("p b d -> p (b d)")).then_inc(f_staged, 1)

            def turn_feats(b, s):
                act.wait_ge(fT_summed, b + 1)
                nc.scalar.copy(fT[s], fT_ps).then_inc(fT_ready, 1)

            def copy_product(b, s):
                act.wait_ge(multiplied, b + 1)
                nc.scalar.copy(G[:, ds(b, 1), :].rearrange("p b d -> p (b d)"), prod_ps[s]).then_inc(prod_copied, 1)

            def feats_step(b, s):
                if not isinstance(b, int) or b > 0:
                    copy_product(b - 1, 1 - s)
                if not isinstance(b, int) or b + 1 < NB:
                    turn_feats(b + 1, 1 - s)
                if not isinstance(b, int) or b + 2 < NB:
                    stage_feats(b + 2)

            def share(b, first, n):
                return range((b - first) * NWT // n, (b - first + 1) * NWT // n)

            act.wait_ge(bases_ready, 1)
            for t in range(NWT):
                at = (spare[:, 0:NROW].rearrange("p (h r) -> p h r", h=2), banks[:, 1:3, 0:NROW // 2], banks[:, 6:8, 0:NROW // 2])[t % 3]
                count_below(at, bases_ps, below[:, 0, t:t + 1], signs[:, 0, t:t + 1])
                if t % 3 == 2:
                    act.drain()
            act.drain().then_inc(rows_counted, 1)
            act.wait_ge(feats_in, 48)
            stage_feats(0)
            turn_feats(0, 0)
            stage_feats(1)
            for b in range(2):
                feats_step(b, b)
            with act.Fori(1, B_FOUND[0] // 2) as i:
                for s in range(2):
                    feats_step(i * 2 + s, s)
            act.wait_ge(found_in, 16 * NWT)
            first, n = B_FOUND
            for b in range(first, first + n):
                feats_step(b, b % 2)
                for t in share(b, first, n):
                    count_below(found[:, t, :], found[:, t, :], below[:, 0, t:t + 1], signs[:, 1, t:t + 1])
            act.drain().then_inc(found_counted, 1)
            with act.Fori((first + n) // 2, B_WINDOW[0] // 2) as i:
                for s in range(2):
                    feats_step(i * 2 + s, s)
            act.wait_ge(dst_w_in, 16 * NWT)

            def count_window(t):
                tile = dst_w[:, ds(t, 1), :].rearrange("p t c -> p (t c)")
                act.drain()
                for m in range(3):
                    count_below(spare[:, m * P:(m + 1) * P], tile, below[:, m, ds(t, 1)], signs[:, 2 + m, ds(t, 1)])

            first, n = B_WINDOW
            for b in range(first, first + n):
                feats_step(b, b % 2)
                for t in share(b, first, n):
                    count_window(t)
            act.drain().then_inc(window_counted, 1)
            with act.Fori((first + n) // 2, NB // 2 - 1) as i:
                for s in range(2):
                    feats_step(i * 2 + s, s)
            for b in range(NB - 3, NB):
                feats_step(b, b % 2)
            copy_product(NB - 1, (NB - 1) % 2)

            act.wait_ge(deg_clipped, 1)
            nc.scalar.activation(rs_out[:, :], degs[:, 0, :], ACT.Sqrt).then_inc(deg_root, 1)
            def upper_part(j):
                act.wait_ge(res_out[j], 16)
                for b in range(j * BLK7, (j + 1) * BLK7):
                    m = nc.scalar.activation(parts[:, b, D:2 * D], G[:, b, 0:D], ACT.Copy, scale=rs_out[:, b:b + 1])
                m.then_inc(upper_ready, 1)

            for t in range(0, NWT, 4):
                n = min(4, NWT - t)
                for m, v in enumerate((edge_lo, edge_v)):
                    act.wait_ge(digits_turned, 2 * (t // 4) + m + 1)
                    nc.scalar.copy(v[:, t * P:(t + n) * P].rearrange("p (t n) -> p t n", t=n), turned_ps[m][:, 0:n, :]).then_inc(edges_ready, 1)
            act.wait_ge(deg_clipped, 2)
            nc.scalar.activation(rs_in[:, :], rs_in[:, :], ACT.Sqrt).then_inc(deg_root, 1)
            act.wait_ge(rs_ready, 1)
            act.drain()
            for j in range(NPC):
                upper_part(j)

            act.wait_ge(general_ready, 1)
            is_general = act.value_load(general[0:1, 0:1], min_val=0, max_val=1)
            with act.If(is_general > 0):
                act.wait_ge(deg_clipped, 3)
                nc.scalar.activation(rs_in[:, 0:NB], degs[:, 1, :], ACT.Sqrt).then_inc(deg_root, 1)

            def evacuate(n, h, i):
                if i == 0:
                    act.wait_ge(summed, n + 1)
                act.wait_ge(general_ready, 1)
                act.wait_ge(built, n * BPB + (i + OHB + 1))
                nc.scalar.copy(counts[h][:, :, i * WB * WN:(i + 1) * WB * WN].rearrange("p b (h w) -> p h w b", h=2),
                               built_ps[i % 2][:, :, 0:WB * WV // 2].rearrange("p h (w b) -> p h w b", b=NB)).then_inc(evacuated, 1)

            def turn_x(j, nb):
                act.wait_ge(x_turned, j + 1)
                nc.scalar.copy(xTp[:, 0:nb], xT_ps[:, 0:nb]).then_inc(xT_ready, 1)

            def gate_exp(j, s, nb):
                act.wait_ge(gap_ready, j + 1)
                nc.scalar.activation(egap[:, s, 0:nb], gap[:, s, 0:nb], ACT.Exp).then_inc(egap_ready, 1)

            def step(j, s):
                before_it = not isinstance(j, int) or j > 0
                for h in range(2):
                    for i in range(BPB):
                        evacuate(j * 2 + (h + 1), 1 - h, i)
                        if (h, i) == (0, 1) and before_it:
                            turn_x(j - 1, 2)
                        if (h, i) == (1, 1) and before_it:
                            gate_exp(j - 1, 1 - s, 2)

            act.drain()
            nc.scalar.preload_act_table(ACT.Exp)
            for i in range(BPB):
                evacuate(0, 0, i)
            for j in range(2):
                step(j, j)
            with act.Fori(1, NPAIR // 2) as i:
                for s in range(2):
                    step(i * 2 + s, s)
            turn_x(NPAIR - 1, 2)
            gate_exp(NPAIR - 1, (NPAIR - 1) % 2, 2)
            turn_x(NPAIR, 1)
            gate_exp(NPAIR, NPAIR % 2, 1)

            act.dma_start(b1_s, b1).then_inc(b1_in, 16)
            act.wait_ge(b1_turned, 1)
            nc.scalar.copy(b1T[:, :, :], bank[7][:, 0:HK * NEXP].rearrange("p (k e) -> p k e", k=HK)).then_inc(b1_ready, 1)
            act.wait_ge(tiles_ready, 1)
            act.drain()
            last = act.value_load(last_i[0:1, 0:1], min_val=1, max_val=TMAX)
            nc.scalar.preload_act_table(ACT.Gelu)

            def turned(t, s):
                act.wait_ge(h_done, t + 1)
                act.wait_ge(tx_done, t + (RING + 1))
                nc.scalar.copy(xT[:, s % 2], tx_ps[s % 2]).then_inc(tx_ready, 1)

            def gelu(t, s):
                code = act.value_load(tile_i[0:1, 0, ds(t, 1)], min_val=0, max_val=(8 * NEXP * RING) - 1)
                e = act.snap((code >> CE) & (NEXP - 1))
                act.wait_ge(tile_done, t + (RING - 1))
                act.wait_ge(b1_ready, 1)
                act.wait_ge(hT_done, t + 3)
                for k in range(HK):
                    nc.scalar.activation(h1[:, s % 2, k, :], hT_ps[s % 2][:, k, :], ACT.Gelu,
                                         bias=b1T[:, k, ds(e, 1)]).then_inc(h1_ready, 1)

            turned(0, 0)
            turned(1, 1)
            with act.Fori(0, TLOOP // RING) as i:
                for s in range(1, RING + 1):
                    t = i * RING + s
                    with act.If(t < last):
                        turned(t + 1, s + 1)
                        gelu(t - 1, s - 1)
                    with act.Else():
                        with act.If(t < last + 1):
                            gelu(t - 1, s - 1)

            for g in range(NFG + 1):
                act.wait_ge(centred, g + 1)
                if g >= 2:
                    act.wait_ge(sq_used, g - 1)
                q, n = (P, BPG) if g < NFG else (TAIL, 1)
                nc.scalar.activation(sqbuf[0:q, g % 2, 0:n], F[0:q, g * BPG:g * BPG + n, :], ACT.Square).then_inc(squared, 1)
            act.wait_ge(var_ready, 1)
            nc.scalar.activation(scale[:, :], mean[:, :], ACT.Sqrt, bias=eps_c[:, :]).then_inc(root_ready, 1)
            for g in range(NFG + 1):
                q, n = (P, BPG) if g < NFG else (TAIL, 1)
                act.wait_ge(lnvar_ready, g + 1)
                nc.scalar.activation(inv[0:q, 0:n], moments[0:q, 0:n, 1], ACT.Sqrt, bias=eps_c[0:q, :]).then_inc(lnroot_ready, 1)

        @block.tensor
        def _(pe):
            pe.wait_ge(consts, 1)
            pe.sem_inc(hist_used, 2)
            pe.sem_inc(built, OHB)
            pe.sem_inc(summed, 2)
            pe.sem_inc(tx_done, RING)
            pe.sem_inc(tile_done, RING)
            pe.sem_inc(h_done, 2)
            pe.sem_inc(hT_done, 2)

            pe.wait_ge(bases_float, 1)
            for m in range(2):
                last = pe.matmul(bases_ps[:, m, :], onesf[0:1, :], bases_f[:, m * (NROW // 2):(m + 1) * (NROW // 2)], start=True, stop=True)
            last.then_inc(bases_ready, 1)

            def count(g, s):
                pe.wait_ge(hist_ready, g + 1)
                for c in range(HC):
                    last = pe.matmul(hist_ps, hist_lo[s][:, :, c], hist_hi[s][:, :, c], start=False, stop=False, skip_group_check=True)
                last.then_inc(hist_used, 1)

            def turn_feats(b):
                if not isinstance(b, int) or b > 0:
                    pe.wait_ge(weights_in, NW)
                    pe.wait_ge(fT_ready, b)
                pe.wait_ge(weights_in, NW)
                pe.wait_ge(f_staged, b + 1)
                for k in range(K):
                    m = pe.transpose(fT_ps[:, k, :], fblk[:, k * P:(k + 1) * P], ident[:, :])
                m.then_inc(fT_summed, 1)

            def multiply(b, s):
                pe.wait_ge(bias_ready, 1)
                pe.wait_ge(fT_ready, b + 1)
                pe.wait_ge(prod_copied, b + 1)
                for m in range(2):
                    for k in range(K):
                        last = pe.matmul(prod_ps[s][:, m * D:(m + 1) * D], fT[s][:, k, :], Wx_s[:, k, m, :], start=(k == 0), stop=(m == 0 and k == K - 1))
                last = pe.matmul(prod_ps[s][:, D:2 * D], onesf[0:1, :], bias_x[0:1, 0, :], start=False, stop=True)
                last.then_inc(multiplied, 1)

            def feats_step(b, s):
                counted = not isinstance(b, int) or b < NHG // 2 - LEAD
                if not isinstance(b, int) or b + 1 < NB:
                    turn_feats(b + 1)
                if counted:
                    count(b * 2 + 2 * LEAD, 0)
                multiply(b, s)
                if counted:
                    count(b * 2 + (2 * LEAD + 1), 1)

            pe.matmul(hist_ps, zeros[:, 0:P], zeros[:, 0:NB], start=True, stop=False, skip_group_check=True)
            with pe.Fori(0, LEAD) as i:
                for s in range(2):
                    count(i * 2 + s, s)
            pe.wait_ge(weights_in, NW)
            turn_feats(0)
            with pe.Fori(0, (NHG // 2 - LEAD) // 2) as i:
                for s in range(2):
                    feats_step(i * 2 + s, s)
            for b in range((NHG // 2 - LEAD) // 2 * 2, NHG // 2 - LEAD):
                feats_step(b, b % 2)
            count(NHG - 1, 0)
            for b in range(NHG // 2 - LEAD, NB):
                feats_step(b, b % 2)
            pe.matmul(hist_ps, zeros[:, 0:P], zeros[:, 0:NB], start=False, stop=True, skip_group_check=True).then_inc(hist_done, 1)

            pe.wait_ge(digits_ready, 1)
            for t in range(0, NWT, 4):
                for m, v in enumerate((low_w, rel_w)):
                    if t > 0:
                        pe.wait_ge(edges_ready, 2 * (t // 4 - 1) + m + 1)
                    for q in range(min(4, NWT - t)):
                        last = pe.transpose(turned_ps[m][:, q, :], v[:, t + q, :], ident[:, :])
                    last.then_inc(digits_turned, 1)
            pe.wait_ge(deg_ready, 1)
            for h in range(2):
                for s in range(WN):
                    pe.matmul(small[:, h * 32:h * 32 + NWT], pick[:, h * WN + s, :], deg_w[:, s, :], start=(s == 0), stop=(s == WN - 1))
            pe.matmul(small[0:1, 64:65], held[:, :], onesf[:, 0:1], start=True, stop=True).then_inc(deg_placed, 1)

            pe.wait_ge(general_ready, 1)
            is_general = pe.value_load(general[0:1, 0:1], min_val=0, max_val=1)
            with pe.If(is_general > 0):
                with pe.Fori(0, NSG) as g:
                    gathered = pe.to_reg(g * (16 * SC) + 16 * SC)
                    pe.wait_ge(general_ready, 1)
                    pe.wait_ge(slow_rows_in, gathered)
                    with pe.Fori(0, NB) as b:
                        pe.wait_ge(general_ready, 1)
                        pe.wait_ge(slow_hot_ready, g * NB + (b + 1))
                        for c in range(SC):
                            pe.matmul(slow_ps[:, 0:D], slow_hot[:, c, :], slow_rows[:, c, :], start=(c == 0), stop=(c == SC - 1))
                        for c in range(SC):
                            last = pe.matmul(slow_ps[:, D:D + 1], slow_hot[:, c, :], onesf[:, 0:1], start=(c == 0), stop=(c == SC - 1))
                        last.then_inc(slow_summed, 1)

            def build(n, i):
                pe.wait_ge(general_ready, 1)
                pe.wait_ge(onehot_ready, n * BPB + (i + 1))
                pe.wait_ge(evacuated, n * BPB + (i + 1))
                for w in range(WB):
                    at = (w % 4) * WV
                    last = pe.matmul(built_ps[i % 2][:, w // 4, at:at + WV], oh_lo[i % OHB][:, :, w], oh_v[i % OHB][:, :, w], start=True, stop=True)
                last.then_inc(built, 1)

            def add_up(n, h, q):
                if q == 0:
                    pe.wait_ge(general_ready, 1)
                    pe.wait_ge(evacuated, n * BPB + (BPB + 2))
                    pe.wait_ge(x_made, n + 1)
                for b in fifth(q):
                    if isinstance(n, int) and n == 0 and (b == fifth(q)[0] or b % BLK7 == 0):
                        pe.wait_ge(split, b // BLK7 + 1)
                    last = pe.matmul(agg_ps[h], counts[h][:, b, :], parts[:, b, :], start=(b == 0), stop=(b == NB - 1))
                if q == 4:
                    last.then_inc(summed, 1)

            def turn_x(j, s, nb):
                pe.wait_ge(general_ready, 1)
                pe.wait_ge(x_made, j * 2 + (nb + 2))
                for b in range(nb):
                    for k in range(K):
                        m = pe.transpose(xT_ps[:, b, k, :], pair_x[s][:, b, k * P:(k + 1) * P], ident[:, :])
                m.then_inc(x_turned, 1)

            def score(j, nb):
                pe.wait_ge(general_ready, 1)
                if not isinstance(j, int) or j > 0:
                    pe.wait_ge(slots_ready, j)
                pe.wait_ge(xT_ready, j + 1)
                for b in range(nb):
                    for k in range(K):
                        m = pe.matmul(logit_ps[:, b, :], xTp[:, b, k, :], Wg_s[:, k, :], start=(k == 0), stop=(k == K - 1))
                m.then_inc(logits_done, 1)

            def ranks(j, s, nb, valid):
                pe.wait_ge(general_ready, 1)
                pe.wait_ge(both_ready, j + 1)
                for b in range(nb):
                    pe.matmul(rank_ps[0:valid, b, :], tri_b[0:valid, 0:valid], both[0:valid, s, b, :], start=True, stop=False)
                    if b == 1:
                        pe.matmul(rank_ps[0:valid, b, :], ones_b[:, 0:valid], both[:, s, 0, :], start=False, stop=False)
                    m = pe.matmul(rank_ps[0:valid, b, :], ones_b[:, 0:valid], before[:, s, :], start=False, stop=True)
                m.then_inc(ranks_done, 1)

            def step(j, s):
                before_it = not isinstance(j, int) or j > 0
                for h in range(2):
                    for q in range(5):
                        add_up(j * 2 + h, h, q)
                        for i in range(min(2 * q, BPB), min(2 * q + 2, BPB)):
                            build(j * 2 + (h + 1), i)
                        if before_it:
                            if (h, q) == (0, 0):
                                turn_x(j - 1, 1 - s, 2)
                            if (h, q) == (0, 1):
                                score(j - 1, 2)
                            if (h, q) == (1, 0):
                                ranks(j - 1, 1 - s, 2, P)

            for i in range(BPB):
                build(0, i)
            for j in range(2):
                step(j, j)
            with pe.Fori(1, NPAIR // 2) as i:
                for s in range(2):
                    step(i * 2 + s, s)
            add_up(NB - 1, 0, 0)
            turn_x(NPAIR - 1, (NPAIR - 1) % 2, 2)
            add_up(NB - 1, 0, 1)
            score(NPAIR - 1, 2)
            for q in range(2, 5):
                add_up(NB - 1, 0, q)
            ranks(NPAIR - 1, (NPAIR - 1) % 2, 2, P)
            turn_x(NPAIR, NPAIR % 2, 1)
            score(NPAIR, 1)
            ranks(NPAIR, NPAIR % 2, 1, TAIL)

            pe.wait_ge(b1_in, 16)
            pe.wait_ge(tables_col, 1)
            pe.matmul(small[0:NEXP, 0:1], before[:, (NPAIR + 1) % 2, :], ones_b[:, 0:1], start=True, stop=True).then_inc(tables, 1)
            for k in range(HK):
                m = pe.transpose(bank[7][:, k * NEXP:(k + 1) * NEXP], b1_s[:, k * P:(k + 1) * P], ident[0:NEXP, 0:NEXP])
            m.then_inc(b1_turned, 1)
            pe.wait_ge(tables_col, 2)
            pe.matmul(bank[2][0:NEXP, 0:1], tri_eq[0:NEXP, 0:NEXP], cntc[:, 1:2], start=True, stop=True).then_inc(tables, 1)
            pe.wait_ge(tables_col, 3)
            pe.matmul(bank[2][0:1, 0:TMAX], onesf[0:NEXP, 0:1], ended[:, 0:TMAX], start=True, stop=True)
            pe.matmul(bank[3][0:1, 0:TMAX], cntc[:, 1:2], ended[:, 0:TMAX], start=True, stop=True)
            pe.matmul(bank[5][0:1, 0:TMAX], cntc[:, 3:4], ended[:, 0:TMAX], start=True, stop=True)
            pe.matmul(bank[6][0:1, 0:1], cntc[:, 1:2], onesf[0:NEXP, 0:1], start=True, stop=True).then_inc(tables, 1)

            pe.wait_ge(tiles_ready, 1)
            pe.wait_ge(b1_ready, 1)
            last = pe.value_load(last_i[0:1, 0:1], min_val=1, max_val=TMAX)

            def turn(t, i, s):
                pe.wait_ge(tiles_ready, 1)
                pe.wait_ge(xg_in[s % RING], i * 16 + 16)
                pe.wait_ge(tx_ready, t + 1)
                for k in range(K):
                    m = pe.transpose(tx_ps[s % 2][:, k, :], xg[:, s % RING, k * P:(k + 1) * P], ident[:, :])
                m.then_inc(tx_done, 1)

            def slots_of(t):
                code = pe.value_load(tile_i[0:1, 1, ds(t, 1)], min_val=0, max_val=RING * RING - 1)
                return pe.snap(code & (RING - 1)), pe.snap((code >> CE) & (RING - 1))

            def layer1(t, i, s, ws):
                pe.wait_ge(w_in[s % RING], i * 48 + 48)
                pe.wait_ge(hs_ready, t + 1)
                pe.wait_ge(tiles_ready, 1)
                pe.wait_ge(tx_ready, t + 3)
                for k in range(K):
                    m = pe.matmul(h_ps[s % 2][:, :], xT[:, s % 2, k, :], w1s[:, ds(ws, 1), k, :].rearrange("p s h -> p (s h)"),
                                  start=(k == 0), stop=(k == K - 1))
                m.then_inc(h_done, 1)

            def turn_h(t, s):
                pe.wait_ge(h1_ready, t * HK + HK)
                pe.wait_ge(tiles_ready, 1)
                pe.wait_ge(hs_ready, t + 3)
                for k in range(HK):
                    m = pe.transpose(hT_ps[s % 2][:, k, :], hs[:, s % 2, k * P:(k + 1) * P], ident[:, :])
                m.then_inc(hT_done, 1)

            def layer2(t, s, ws):
                pe.wait_ge(y_ready, t + 1)
                for k in range(HK):
                    pe.wait_ge(tiles_ready, 1)
                    pe.wait_ge(h1_ready, t * HK + (2 * HK + k + 1))
                    m = pe.matmul(y_ps[s % 2], h1[:, s % 2, k, :], w2s[:, ds(ws, 1), k, :].rearrange("p s d -> p (s d)"),
                                  start=(k == 0), stop=(k == HK - 1))
                m.then_inc(tile_done, 1)

            turn(0, 0, 0)
            turn(1, 0, 1)
            ws, _ = slots_of(0)
            layer1(0, 0, 0, ws)
            with pe.Fori(0, TLOOP // RING) as i:
                for s in range(1, RING + 1):
                    t = i * RING + s
                    with pe.If(t < last):
                        ws, ws_before = slots_of(t)
                        turn(t + 1, i + (s + 1) // RING, (s + 1) % RING)
                        turn_h(t - 1, s - 1)
                        layer1(t, i + s // RING, s % RING, ws)
                        layer2(t - 1, s - 1, ws_before)
                    with pe.Else():
                        with pe.If(t < last + 1):
                            ws, ws_before = slots_of(t)
                            turn_h(t - 1, s - 1)
                            layer2(t - 1, s - 1, ws_before)

            def over_nodes(ps, ready, get, used=None):
                pe.matmul(ps, onesf[:, :], zeros[:, :], start=True, stop=False, skip_group_check=True)
                for g in range(NFG + 1):
                    pe.wait_ge(ready, g + 1)
                    q, n = (P, BPG) if g < NFG else (TAIL, 1)
                    for b in range(n):
                        m = pe.matmul(ps, onesf[0:q, :], get(g, b, q), start=False, stop=(g == NFG), skip_group_check=True)
                    if used is not None and g < NFG:
                        m.then_inc(used, 1)
                return m

            def y_at(g, b, q):
                return F[0:q, g * BPG + b, :]

            pe.wait_ge(y_summed, 2)
            pe.matmul(sum_ps, onesf[:, :], zeros[:, :], start=True, stop=False, skip_group_check=True)
            for g in range(NFG + 1):
                pe.wait_ge(y_summed, g + 3)
                q, n = (P, BPG) if g < NFG else (TAIL, 1)
                for b in range(n):
                    m = pe.matmul(sum_ps, onesf[0:q, :], y_at(g, b, q), start=False, stop=(g == NFG), skip_group_check=True)
            m.then_inc(sum_done, 1)
            over_nodes(sq_ps, squared, lambda g, b, q: sqbuf[0:q, g % 2, b, :], sq_used).then_inc(sq_done, 1)

        @block.vector
        def _(dve):
            dve.memset(src_i[:, EC:EW], N)
            dve.memset(padends[:, 0, :], NOWHERE)
            dve.memset(padends[:, 1, :], N)
            dve.memset(G[:, NB - 1, D:2 * D], 0.0).then_inc(tails_set, 1)
            dve.memset(zeros[:, :], 0.0)
            dve.memset(onesf[:, :], 1.0)
            dve.memset(ones_b[:, :], 1.0)
            dve.memset(eps_c[:, :], EPS)
            dve.memset(before[:, :, :], 0.0)
            dve.memset(iota[:, :], 0.0)
            dve.wait_ge(iotas, 1)
            dve.drain()
            dve.tensor_copy(iota[:, 0:P], iota_i[:, :])
            dve.tensor_copy(pcol[:, :], pcol_i[:, :])
            dve.tensor_copy(first_w[:, :], win_i[:, :])
            dve.drain()
            for m in range(3):
                dve.tensor_scalar(below[:, m, :], first_w[:, :], m - 0.5, None, ALU.add)
            dve.tensor_scalar(iota[:, P:192], iota[:, 0:192 - P], float(P), None, ALU.add)
            dve.tensor_scalar(ident[:, :], iota[:, 0:P], pcol[:, :], None, ALU.is_equal)
            dve.wait_ge(bases_in, 32)
            dve.tensor_copy(bases_f[:, :], bases_i[:, :]).then_inc(bases_float, 1)
            dve.drain().then_inc(consts, 1)
            dve.sem_inc(prod_copied, 2)
            dve.sem_inc(evacuated, 2)
            dve.sem_inc(x_made, 2)
            dve.sem_inc(y_ready, 2)
            dve.sem_inc(tx_ready, 2)
            dve.sem_inc(h1_ready, 2 * HK)
            dve.sem_inc(hs_ready, 2)
            dve.sem_inc(y_summed, 2)
            dve.tensor_copy(iota_lo16[:, :, :], iota[:, 0:P].unsqueeze(2).to_broadcast([P, P, HC]))
            dve.tensor_copy(iota_hi16[:, :, :], iota[:, 0:NB].unsqueeze(2).to_broadcast([P, NB, HC]))

            dve.memset(padlist[:, :, 0], N)
            dve.memset(padlist[:, :, 1], 2 * N)
            dve.memset(padlist[:, :, 2:4], 0).then_inc(lists_set, 1)

            dve.wait_ge(src_in, 32)
            src_g = src_i.rearrange("p (g c) -> p g c", g=NHG)
            digit_g = digit_i.rearrange("p (g c) -> p g c", g=NHG)
            dve.tensor_scalar(digit_g, src_g, P - 1, None, ALU.bitwise_and)
            dve.drain()
            dve.tensor_copy(src_lo[:, :, :], digit_g)
            dve.drain()
            dve.tensor_scalar(digit_g, src_g, P.bit_length() - 1, None, ALU.logical_shift_right)
            dve.drain()
            dve.tensor_copy(src_hi[:, :, :], digit_g)
            dve.drain()

            def count(g, s):
                dve.wait_ge(hist_used, g + 1)
                dve.tensor_tensor(hist_lo[s], src_lo[:, ds(g, 1), :].to_broadcast([P, P, HC]), iota_lo16[:, :, :], ALU.is_equal)
                dve.tensor_tensor(hist_hi[s], src_hi[:, ds(g, 1), :].to_broadcast([P, NB, HC]), iota_hi16[:, :, :], ALU.is_equal
                                  ).then_inc(hist_ready, 1)

            def count_pairs(first, end):
                with dve.Fori(first, end) as i:
                    for s in range(2):
                        count(i * 2 + s, s)

            count_pairs(0, 1)
            dve.wait_ge(weights_in, NW)
            dve.tensor_tensor(bias_x[:, 0, :], bias_x[:, 0, :], bias_x[:, 1, :], ALU.add)
            dve.drain().then_inc(bias_ready, 1)
            count_pairs(1, G_ROW)
            dve.wait_ge(rows_counted, 1)
            dve.tensor_scalar(signs[:, 0, :], signs[:, 0, :], 0.5, NROW / 2 - 1.0, ALU.mult, ALU.add)
            dve.drain()
            dve.tensor_scalar(row_w[:, :], signs[:, 0, :], 0.0, None, ALU.max)
            dve.drain().then_inc(row_ready, 1)
            count_pairs(G_ROW, G_EDGE)
            dve.wait_ge(found_counted, 1)
            dve.tensor_scalar(signs[:, 0, :], row_w[:, :], float(ROW), ROW / 2.0, ALU.mult, ALU.add)
            dve.drain()
            dve.scalar_tensor_tensor(edge_w[:, :], signs[:, 1, :], 0.5, signs[:, 0, :], ALU.mult, ALU.add)
            dve.drain().then_inc(edge_ready, 1)
            count_pairs(G_EDGE, G_DIGITS)
            dve.tensor_copy(iota_lo[:, :, :], iota[:, 0:P].unsqueeze(2).to_broadcast([P, P, WB]))
            dve.tensor_copy(iota_v[:, :, :], iota[:, 0:WV].unsqueeze(2).to_broadcast([P, WV, WB]))
            dve.tensor_scalar(tri_b[:, :], iota[:, 0:P], pcol[:, :], None, ALU.is_gt)
            dve.tensor_scalar(tri_eq[:, :], iota[:, 0:P], pcol[:, :], None, ALU.is_ge)
            for m in range(4):
                dve.tensor_scalar(pcols[:, m:m + 1], pcol[:, :], float(WN), float(m % WN - (m // WN) * P), ALU.mult, ALU.add)
            dve.drain()
            for m in range(4):
                dve.tensor_scalar(pick[:, m, :], iota[:, 0:P], pcols[:, m:m + 1], 0.5, ALU.is_equal, ALU.mult)
            dve.wait_ge(window_counted, 1)
            dve.wait_ge(src_w_in, 16 * NWT)
            dve.tensor_scalar(hi_w, src_w, P.bit_length() - 1, None, ALU.logical_shift_right)
            dve.tensor_tensor(rel_w, dst_w, first_w[:, :].unsqueeze(2).to_broadcast([P, NWT, P]), ALU.subtract)
            dve.drain()
            dve.scalar_tensor_tensor(low_w, hi_w, float(-P), src_w, ALU.mult, ALU.add)
            dve.scalar_tensor_tensor(rel_w, rel_w, float(NB), hi_w, ALU.mult, ALU.add)
            dve.drain().then_inc(digits_ready, 1)
            dve.tensor_tensor(deg_w[:, :, :], signs[:, 3:5, :], signs[:, 2:4, :], ALU.subtract)
            dve.drain()
            dve.tensor_reduce(held[:, :], deg_w[:, :, :], AX.XY, ALU.add)
            dve.drain().then_inc(deg_ready, 1)
            count_pairs(G_DIGITS, NHG // 2)
            count(NHG - 1, 0)
            dve.wait_ge(hist_done, 1)
            dve.tensor_scalar(degs[:, 0, :], hist_ps, 1.0, None, ALU.max).then_inc(deg_clipped, 1)
            dve.wait_ge(deg_root, 1)
            dve.reciprocal(rs_out[:, :], rs_out[:, :])
            dve.drain().then_inc(rs_ready, 1)
            dve.wait_ge(deg_placed, 1)
            dve.tensor_scalar(rs_in[:, :].rearrange("p (t h) -> p h t", h=2), small[:, 0:64].rearrange("p (h t) -> p h t", h=2)[:, :, 0:NWT],
                              1.0, None, ALU.max).then_inc(deg_clipped, 1)
            dve.tensor_scalar(general_f[:, :], small[0:1, 64:65], 2.0 * E, None, ALU.is_lt)
            dve.drain()
            dve.tensor_copy(general[:, :], general_f[:, :])
            dve.drain().then_inc(general_ready, 1)

            def lower_part(j):
                dve.wait_ge(upper_ready, j + 1)
                for b in range(j * BLK7, (j + 1) * BLK7):
                    m = dve.scalar_tensor_tensor(parts[:, b, 0:D], G[:, b, 0:D], rs_out[:, b:b + 1], parts[:, b, D:2 * D].bitcast(F32),
                                                 ALU.mult, ALU.subtract)
                m.then_inc(split, 1)

            dve.wait_ge(deg_root, 2)
            dve.reciprocal(rs_in[:, :], rs_in[:, :])
            dve.wait_ge(edges_ready, 2 * -(-NWT // 4))
            dve.drain()

            def one_hots(n, i):
                first = n * WPB + i * WB
                dve.wait_ge(built, n * BPB + (i + 1))
                dve.tensor_tensor(oh_lo[i % OHB], edge_lo[:, ds(first, WB)].unsqueeze(1).to_broadcast([P, P, WB]), iota_lo[:, :, :], ALU.is_equal)
                dve.tensor_tensor(oh_v[i % OHB], edge_v[:, ds(first, WB)].unsqueeze(1).to_broadcast([P, WV, WB]), iota_v[:, :, :], ALU.is_equal
                                  ).then_inc(onehot_ready, 1)

            is_general = dve.value_load(general[0:1, 0:1], min_val=0, max_val=1)
            with dve.If(is_general > 0):
                for j in range(NPC):
                    lower_part(j)
                dve.drain()
                for j in range(NPC):
                    if j >= 2:
                        dve.wait_ge(piece_out[j % 2], 16 * (j // 2))
                    b = slice(j * BLK7, (j + 1) * BLK7)
                    dve.tensor_tensor(piece[j % 2], parts[:, b, 0:D].bitcast(F32), parts[:, b, D:2 * D].bitcast(F32), ALU.add
                                      ).then_inc(piece_ready, 1)
                for s in range(2):
                    dve.wait_ge(piece_out[s], 16 * sum(j % 2 == s for j in range(NPC)))
                dve.memset(slow_sums, 0.0)
                dve.memset(degs[:, 1, :], 0.0)
                dve.drain().then_inc(slow_used, 1)
                with dve.Fori(0, NSG) as g:
                    dve.wait_ge(slow_edges_in, g * 32 + 32)
                    dve.tensor_copy(slow_rel[:, :], slow_dst[:, :])
                    dve.drain()
                    with dve.Fori(0, NB) as b:
                        dve.tensor_tensor(slow_hot, slow_rel[:, :].unsqueeze(2).to_broadcast([P, SC, P]),
                                          iota[:, 0:P].unsqueeze(1).to_broadcast([P, SC, P]), ALU.is_equal).then_inc(slow_hot_ready, 1)
                        dve.wait_ge(slow_summed, g * NB + (b + 1))
                        sums_b = slow_sums[:, ds(b, 1), :].rearrange("p b d -> p (b d)")
                        dve.tensor_tensor(sums_b, sums_b, slow_ps[:, 0:D], ALU.add)
                        dve.tensor_tensor(degs[:, 1, ds(b, 1)], degs[:, 1, ds(b, 1)], slow_ps[:, D:D + 1], ALU.add)
                        dve.tensor_scalar(slow_rel[:, :], slow_rel[:, :], float(-P), None, ALU.add)
                        dve.drain()
                    dve.drain().then_inc(slow_used, 1)
                dve.tensor_scalar(degs[:, 1, :], degs[:, 1, :], 1.0, None, ALU.max).then_inc(deg_clipped, 1)
                dve.wait_ge(deg_root, 3)
                dve.reciprocal(rs_in[:, 0:NB], rs_in[:, 0:NB])
                dve.drain()
                with dve.Fori(0, NB) as b:
                    dve.wait_ge(slow_res_in, b * 16 + 16)
                    dve.scalar_tensor_tensor(fblk, slow_sums[:, ds(b, 1), :].rearrange("p b d -> p (b d)"), rs_in[:, ds(b, 1)], fblk,
                                             ALU.mult, ALU.add).then_inc(slow_added, 1)
                dve.memset(edge_v, -1.0)
                dve.drain()
                for i in range(BPB):
                    one_hots(0, i)
            with dve.Else():
                for i in range(BPB):
                    one_hots(0, i)
                for j in range(NPC):
                    lower_part(j)

            def make_x(n, j, s, h, half):
                dve.wait_ge(summed, n + 3)
                dve.wait_ge(res_in[s], half * 16 + 16)
                if not isinstance(j, int) or j >= 2:
                    dve.wait_ge(x_out[s], half * 16)
                at, rs = pair_x[s][:, h, :], rs_in[:, ds(n, 1)]
                dve.scalar_tensor_tensor(at, agg_ps[h][:, 0:D], rs, res_buf[s][:, h, :], ALU.mult, ALU.add)
                dve.drain()
                dve.scalar_tensor_tensor(at, agg_ps[h][:, D:2 * D], rs, at, ALU.mult, ALU.add).then_inc(x_made, 1)

            def choose(j, s, nb, valid):
                dve.wait_ge(logits_done, j + 1)
                dve.tensor_tensor(logit[:, 0:nb], logit_ps[:, 0:nb], bg_s[:, :].unsqueeze(1).to_broadcast([P, nb, NEXP]), ALU.add)
                dve.drain()
                for b in range(nb):
                    dve.max(top8[:, b, :], logit[:, b, :])
                dve.drain()
                for b in range(nb):
                    dve.max_index(top8i[:, b, :], top8[:, b, :], logit[:, b, :])
                dve.tensor_tensor(gap[:, s, 0:nb], top8[:, 0:nb, 1], top8[:, 0:nb, 0], ALU.subtract).then_inc(gap_ready, 1)
                dve.drain()
                dve.tensor_copy(expert[:, s, 0:nb], top8i[:, 0:nb, 0:2])
                dve.drain()
                for b in range(nb):
                    dve.tensor_tensor(picks[:, s, b], expert[:, s, b].unsqueeze(2).to_broadcast([P, 2, NEXP]),
                                      iota[:, 0:NEXP].unsqueeze(1).to_broadcast([P, 2, NEXP]), ALU.is_equal)
                dve.drain()
                dve.tensor_tensor(both[:, s, 0:nb], picks[:, s, 0:nb, 0], picks[:, s, 0:nb, 1], ALU.add)
                dve.drain().then_inc(both_ready, 1)
                if not isinstance(j, int) or j > 0:
                    dve.wait_ge(ranks_done, j)
                dve.tensor_copy(before[:, 1 - s, :], before[:, s, :])
                dve.drain()
                dve.tensor_tensor(before[0:valid, 1 - s, :], before[0:valid, 1 - s, :], both[0:valid, s, 0, :], ALU.add)
                if nb == 2:
                    dve.drain()
                    dve.tensor_tensor(before[:, 1 - s, :], before[:, 1 - s, :], both[:, s, 1, :], ALU.add)

            def place(j, s, nb):
                dve.wait_ge(ranks_done, j + 1)
                for b in range(nb):
                    dve.tensor_tensor(ranked[:, b], picks[:, s, b], rank_ps[:, b, :].unsqueeze(1).to_broadcast([P, 2, NEXP]), ALU.mult)
                dve.drain()
                dve.tensor_reduce(rank[:, 0:nb], ranked[:, 0:nb], AX.X, ALU.add)
                dve.drain()
                dve.tensor_scalar(over[:, 0:nb], rank[:, 0:nb], float(CAP), float(NSLOT), ALU.is_ge, ALU.mult)
                dve.scalar_tensor_tensor(slot_f[:, 0:nb], expert[:, s, 0:nb], float(LROWS), rank[:, 0:nb], ALU.mult, ALU.add)
                dve.wait_ge(egap_ready, j + 1)
                dve.tensor_scalar(gap[:, s, 0:nb], egap[:, s, 0:nb], 1.0, None, ALU.add)
                dve.drain()
                if not isinstance(j, int) or j >= 2:
                    dve.wait_ge(list_out[s], list_before(j, s))
                dve.tensor_tensor(slot[:, s, 0:nb], slot_f[:, 0:nb], over[:, 0:nb], ALU.add)
                gates = entry[:, s, 0:nb, :, 2].bitcast(F32)
                dve.reciprocal(gates[:, :, 0], gap[:, s, 0:nb])
                dve.drain()
                dve.tensor_tensor(gates[:, :, 1], gates[:, :, 0], egap[:, s, 0:nb], ALU.mult)
                dve.tensor_copy(entry[:, s, 0:nb, :, 0:2].rearrange("p b k c -> p (b k) c"),
                                tok_view(j, nb))
                dve.drain().then_inc(slots_ready, 1)

            def tok_view(j, nb):
                return tok_i[:, ds(j * 2, nb), :, :].rearrange("p b k c -> p (b k) c")

            def list_before(j, s):
                n = (j - s) // 2 if isinstance(j, int) else j_half[0]
                return n * 64

            j_half = [0]

            def step(j, s, half):
                after, first = j - 1, isinstance(j, int) and j == 0
                half_after = after // 2 if isinstance(j, int) else (half if s == 1 else half - 1)
                if not first:
                    make_x(j * 2 - 1, after, 1 - s, 1, half_after)
                for i in range(4, 6):
                    one_hots(j * 2 + 1, i)
                if not first:
                    choose(after, 1 - s, 2, P)
                for i in range(6, 8):
                    one_hots(j * 2 + 1, i)
                for i in range(0, 2):
                    one_hots(j * 2 + 2, i)
                make_x(j * 2, j, s, 0, j // 2 if isinstance(j, int) else half)
                for i in range(2, 6):
                    one_hots(j * 2 + 2, i)
                if not first:
                    j_half[0] = half_after
                    place(after, 1 - s, 2)
                for i in range(6, 8):
                    one_hots(j * 2 + 2, i)
                if not isinstance(j, int) or j < NPAIR - 1:
                    for i in range(4):
                        one_hots(j * 2 + 3, i)

            dve.wait_ge(iotas, 2)
            dve.memset(entry[:, :, :, :, :], 0)
            for i in range(4):
                one_hots(1, i)
            for j in range(2):
                step(j, j, None)
            with dve.Fori(1, NPAIR // 2 - 1) as i:
                for s in range(2):
                    step(i * 2 + s, s, i)
            for j in range(NPAIR - 2, NPAIR):
                step(j, j % 2, None)
            make_x(NB - 2, NPAIR - 1, (NPAIR - 1) % 2, 1, (NPAIR - 1) // 2)
            choose(NPAIR - 1, (NPAIR - 1) % 2, 2, P)
            make_x(NB - 1, NPAIR, NPAIR % 2, 0, NPAIR // 2)
            place(NPAIR - 1, (NPAIR - 1) % 2, 2)
            choose(NPAIR, NPAIR % 2, 1, TAIL)
            place(NPAIR, NPAIR % 2, 1)

            dve.drain().then_inc(tables_col, 1)
            dve.wait_ge(tables, 1)
            dve.tensor_scalar(cntc[:, 0:1], small[0:NEXP, 0:1], float(CAP), float(P - 1), ALU.min, ALU.add)
            dve.drain()
            dve.tensor_copy(cnti[:, 0:1], cntc[:, 0:1])
            dve.drain()
            dve.tensor_scalar(cnti[:, 1:2], cnti[:, 0:1], P.bit_length() - 1, None, ALU.logical_shift_right)
            dve.drain()
            dve.tensor_copy(cntc[:, 1:2], cnti[:, 1:2])
            dve.drain()
            dve.tensor_scalar(cntc[:, 3:4], cntc[:, 1:2], 0.0, None, ALU.is_gt)
            dve.drain().then_inc(tables_col, 1)
            dve.wait_ge(tables, 2)
            dve.tensor_copy(cntc[:, 2:3], bank[2][0:NEXP, 0:1])
            dve.drain()
            dve.tensor_scalar(ended[:, :], iota[0:NEXP, :], cntc[:, 2:3], None, ALU.is_ge)
            dve.drain().then_inc(tables_col, 1)
            dve.wait_ge(tables, 3)
            T = slice(0, TMAX)
            dve.tensor_tensor(tile_f[:, 0, T], iota[0:1, T], bank[3][0:1, T], ALU.subtract)
            dve.tensor_copy(tile_i[:, 1, T], bank[5][0:1, T])
            dve.drain()
            dve.tensor_scalar(tile_i[:, 1, T], tile_i[:, 1, T], RING - 1, None, ALU.bitwise_and)
            dve.scalar_tensor_tensor(tile_f[:, 1, T], tile_f[:, 0, T], float(NEXP), bank[2][0:1, T], ALU.mult, ALU.add)
            dve.drain()
            dve.tensor_copy(tile_f[:, 2, T], tile_i[:, 1, T])
            dve.drain()
            dve.scalar_tensor_tensor(tile_f[:, 3, T], tile_f[:, 1, T], float(RING), tile_f[:, 2, T], ALU.mult, ALU.add)
            dve.drain()
            dve.tensor_copy(tile_i[:, 0, T], tile_f[:, 3, T])
            dve.scalar_tensor_tensor(tile_f[:, 0, 1:TMAX], tile_f[:, 2, 0:TMAX - 1], float(RING), tile_f[:, 2, 1:TMAX], ALU.mult, ALU.add)
            dve.tensor_copy(tile_f[:, 0, 0:1], tile_f[:, 2, 0:1])
            dve.drain()
            dve.tensor_copy(tile_i[:, 1, T], tile_f[:, 0, T])
            dve.tensor_copy(last_i[:, :], bank[6][0:1, 0:1])
            dve.drain().then_inc(tiles_ready, 1)

            dve.drain()
            last = dve.value_load(last_i[0:1, 0:1], min_val=1, max_val=TMAX)

            def copy_h(t, s):
                dve.wait_ge(hT_done, t + 1)
                dve.wait_ge(h_done, t + 3)
                dve.tensor_copy(hs[:, s % 2, :], h_ps[s % 2][:, :]).then_inc(hs_ready, 1)

            def result(t, i, s):
                code = dve.value_load(tile_i[0:1, 0, ds(t, 1)], min_val=0, max_val=(8 * NEXP * RING) - 1)
                ws = dve.snap(code & (RING - 1))
                dve.wait_ge(y_out[s], i * 16 + 16)
                dve.wait_ge(tile_done, t + (RING + 1))
                dve.tensor_tensor(yo[:, s, :], y_ps[s % 2], b2s[:, ds(ws, 1), :].rearrange("p s d -> p (s d)"), ALU.add)
                dve.drain()
                dve.tensor_scalar(yo[:, s, :], yo[:, s, :], lt[:, s, 2:3].bitcast(F32), None, ALU.mult).then_inc(y_ready, 1)

            copy_h(0, 0)
            with dve.Fori(0, TLOOP // RING) as i:
                for s in range(1, RING + 1):
                    t = i * RING + s
                    with dve.If(t < last):
                        copy_h(t, s)
                        result(t - 1, i, s - 1)
                    with dve.Else():
                        with dve.If(t < last + 1):
                            result(t - 1, i, s - 1)

            dve.wait_ge(x_in, 16)
            for g in range(NFG + 1):
                q, n = (P, BPG) if g < NFG else (TAIL, 1)
                Fg = F[0:q, g * BPG:g * BPG + n, :]
                dve.wait_ge(y_in[g % 2], 16 * (g // 2 + 1))
                dve.tensor_tensor(Fg, Fg, ybuf[0:q, g % 2, 0:n, 0], ALU.add)
                dve.drain()
                dve.tensor_tensor(Fg, Fg, ybuf[0:q, g % 2, 0:n, 1], ALU.add).then_inc(y_summed, 1)
            dve.wait_ge(sum_done, 1)
            dve.tensor_scalar(mean[:, :], sum_ps, 1.0 / N, None, ALU.mult)
            dve.drain()
            for g in range(NFG + 1):
                q, n = (P, BPG) if g < NFG else (TAIL, 1)
                Fg = F[0:q, g * BPG:g * BPG + n, :]
                dve.tensor_tensor(Fg, Fg, mean[0:q, :].unsqueeze(1).to_broadcast([q, n, D]), ALU.subtract).then_inc(centred, 1)
            dve.wait_ge(sq_done, 1)
            dve.tensor_scalar(mean[:, :], sq_ps, 1.0 / N, None, ALU.mult).then_inc(var_ready, 1)
            dve.wait_ge(root_ready, 1)
            dve.reciprocal(scale[:, :], scale[:, :])
            dve.drain()
            dve.tensor_tensor(scale[:, :], scale[:, :], gb_s[:, 0, :], ALU.mult)
            dve.drain()
            for g in range(NFG + 1):
                q, n = (P, BPG) if g < NFG else (TAIL, 1)
                Fg = F[0:q, g * BPG:g * BPG + n, :]
                dve.tensor_tensor(Fg, Fg, scale[0:q, :].unsqueeze(1).to_broadcast([q, n, D]), ALU.mult)
                dve.wait_ge(f_ready, g + 1)
                dve.drain()
                dve.tensor_tensor(Fg, Fg, fbuf[0:q, g % 2, 0:n], ALU.add).then_inc(f_used, 1)
                dve.drain()
                for b in range(n):
                    dve.bn_stats(stats[0:q, b, :], F[0:q, g * BPG + b, :])
                dve.drain()
                for b in range(n):
                    dve.bn_aggr(moments[0:q, b, :], stats[0:q, b, :])
                dve.drain().then_inc(lnvar_ready, 1)
                dve.wait_ge(lnroot_ready, g + 1)
                dve.reciprocal(inv[0:q, 0:n], inv[0:q, 0:n])
                dve.drain()
                for b in range(n):
                    m = dve.tensor_scalar(F[0:q, g * BPG + b, :], F[0:q, g * BPG + b, :], moments[0:q, b, 0:1], inv[0:q, b:b + 1],
                                          ALU.subtract, ALU.mult)
                m.then_inc(out_ready, 1)
                dve.drain()


_INS = ["x", "src", "dst", "L0_gnn_W_gc", "L0_gnn_b_gc", "L0_gnn_W_res", "L0_gnn_b_res", "L0_gnn_Wg", "L0_gnn_bg",
        "L0_gnn_w1", "L0_gnn_b1", "L0_gnn_w2", "L0_gnn_b2", "L0_gnn_gamma", "L0_gnn_beta"]


def kernel(**inputs):
    import numpy as _np
    import concourse.bacc as _bacc
    from concourse import mybir as _mybir
    from concourse.bass_utils import run_bass_kernel_spmd as _run

    nc = _bacc.Bacc("TRN2", target_bir_lowering=False, num_devices=1)
    arrays, args = {}, []
    for name in _INS:
        a = _np.ascontiguousarray(inputs[name])
        arrays[f"in_{name}_dram"] = a
        args.append(nc.dram_tensor(f"in_{name}_dram", a.shape, _mybir.dt.from_np(a.dtype), kind="ExternalInput").ap())
    shape = inputs["x"].shape
    args.append(nc.dram_tensor("out_0_dram", shape, _mybir.dt.float32, kind="ExternalOutput").ap())
    gnn_kernel(nc, *args)
    r = _run(nc, [arrays], core_ids=[0])
    return r.results[0]["out_0_dram"]
```

```python
from contextlib import ExitStack

import concourse.bass as bass
from concourse import mybir

ALU = mybir.AluOpType
ACT = mybir.ActivationFunctionType
AX = mybir.AxisListType
F32 = mybir.dt.float32
F32R = mybir.dt.float32r
BF16 = mybir.dt.bfloat16
I32 = mybir.dt.int32
U32 = mybir.dt.uint32
ds = bass.ds

P = 128
CAP = 1024
EPS = 1e-5
RING = 8
AHEAD = 6
HC = 16
ROW = 256
WN = 2
WB = 8
OHB = 4
NOWHERE = 1 << 20
SC = 8


def gnn_kernel(nc, x, src, dst, W_gc, b_gc, W_res, b_res, Wg, bg, w1, b1, w2, b2, gamma, beta, out):
    N, D = x.shape
    E = src.shape[0]
    NEXP = Wg.shape[1]
    H = w1.shape[2]
    K, HK = D // P, H // P
    NB = -(-N // P)
    NPAD = NB * P
    TAIL = N - (NB - 1) * P
    EC = E // P
    EREST = E - EC * P
    NHG = -(-(EC + 1) // HC)
    LEAD = 3
    FIRST = 6
    NROW = -(-E // ROW)
    RC = -(-NROW // P)
    PADROWS = -(-(NROW * ROW + P) // (P * SC)) * (P * SC) // ROW
    EPAD = PADROWS * ROW
    NSG = EPAD // (P * SC)
    NWT = -(-(NB * P // WN) // P)
    WPB = P // WN
    BPB = WPB // WB
    WV = WN * NB
    LROWS = CAP + P
    NSLOT = NEXP * LROWS
    TMAX = (2 * N + NEXP * (P - 1)) // P + 1
    TLOOP = -(-(TMAX + 1) // RING) * RING
    CE, CJ = RING.bit_length() - 1, (RING * NEXP).bit_length() - 1
    NPAIR = (NB - 1) // 2
    BPG = 8
    NFG = (NB - 1) // BPG
    BLK7 = 7
    NPC = NB // BLK7
    LATE = NPC - 2
    assert NB % BLK7 == 0 and (NB - 1) % (2 * BPG) == 0 and NPAIR * 2 + 1 == NB and NPAIR % 2 == 0
    assert NHG % 2 == 1 and NROW % 2 == 0 and BPB == 2 * OHB and NB % 2 == 1 and NHG // 2 - LEAD < NB and WV * 4 <= 512

    restab = nc.dram_tensor("restab", (NPAD, D), F32, kind="Internal").ap()
    xtab = nc.dram_tensor("xtab", (NPAD, D), F32, kind="Internal").ap()
    htab = nc.dram_tensor("htab", (NPAD, D), F32, kind="Internal").ap()
    srcpad = nc.dram_tensor("srcpad", (PADROWS, ROW), I32, kind="Internal").ap()
    dstpad = nc.dram_tensor("dstpad", (PADROWS, ROW), I32, kind="Internal").ap()
    lists = nc.dram_tensor("lists", (NSLOT, 4), I32, kind="Internal").ap()
    ytab = nc.dram_tensor("ytab", (2 * N + P, D), F32, kind="Internal").ap()
    src_flat = srcpad.rearrange("r c -> (r c)")
    dst_flat = dstpad.rearrange("r c -> (r c)")

    with ExitStack() as ctx:
        def sb(name, shape, dt=F32):
            return ctx.enter_context(nc.sbuf_tensor(name, shape, dt))

        def sem(name):
            return ctx.enter_context(nc.semaphore(name))

        with nc.sbuf_tensor("parts_r", [P, NB * 2 * D], F32R) as parts_r:
            parts = parts_r[:, :].rearrange("p (b d) -> p b d", b=NB)
        big = sb("big", [P, NB * 2 * D])
        G = big[:, :].rearrange("p (b d) -> p b d", b=NB)
        F = big[:, 0:NB * D].rearrange("p (b d) -> p b d", b=NB)
        FB = NB * D
        squares = big[:, FB:2 * FB].rearrange("p (b d) -> p b d", b=NB)

        AW = 2 * NB * P
        EW = NHG * HC
        OHW = max(OHB * WB * (P + WV), 2 * HC * (P + NB) + EW) // 2
        with nc.sbuf_tensor("counts_r", [P, AW], F32R) as counts_r:
            counts = [counts_r[:, h * NB * P:(h + 1) * NB * P].rearrange("p (b n) -> p b n", b=NB) for h in range(2)]
        work = sb("work", [P, AW + OHW])

        def part(at, words):
            return work[:, at:at + words]
        OH1, OH2 = WB * P // 2, WB * WV // 2
        oh_lo = [part(AW + s * OH1, OH1).bitcast(BF16).rearrange("p (v w) -> p v w", w=WB) for s in range(OHB)]
        oh_v = [part(AW + OHB * OH1 + s * OH2, OH2).bitcast(BF16).rearrange("p (v w) -> p v w", w=WB) for s in range(OHB)]
        HB1, HB2 = HC * P // 2, HC * NB // 2
        hist_lo = [part(AW + s * HB1, HB1).bitcast(BF16).rearrange("p (v c) -> p v c", c=HC) for s in range(2)]
        hist_hi = [part(AW + 2 * HB1 + s * HB2, HB2).bitcast(BF16).rearrange("p (v c) -> p v c", c=HC) for s in range(2)]
        src_i = part(0, EW).bitcast(I32)
        digit_i = part(EW, EW).bitcast(I32)
        iota_lo16 = part(2 * EW, HB1).bitcast(BF16).rearrange("p (v c) -> p v c", c=HC)
        iota_hi16 = part(2 * EW + HB1, HB2).bitcast(BF16).rearrange("p (v c) -> p v c", c=HC)
        A1 = 2 * EW + HB1 + HB2
        bases_i = part(A1, 3 * RC).bitcast(I32).rearrange("p (m c) -> p m c", m=3)
        base_f = part(A1 + 3 * RC, 2 * RC).rearrange("p (m c) -> p m c", m=2)
        A4 = A1 + 5 * RC
        base_lo = part(A4, RC * P).rearrange("p (c v) -> p c v", c=RC)
        base_hi = part(A4 + RC * P, RC * NWT).rearrange("p (c v) -> p c v", c=RC)
        A5 = A4 + RC * (P + NWT)
        tri = part(A5, P)
        bins = part(A5 + P, NWT)
        bin_sums = work[0:NWT, A5 + P + NWT:A5 + 2 * P + NWT]
        pick = part(A1, 4 * P).rearrange("p (m n) -> p m n", m=4)
        spare = part(A1 + 4 * P, 3 * P // 2).bitcast(BF16)
        A2 = AW - NWT * ROW
        found = part(A2, NWT * ROW).bitcast(I32).rearrange("p (t c) -> p t c", t=NWT)
        dst_w = part(A2, NWT * P).bitcast(I32).rearrange("p (t c) -> p t c", t=NWT)
        src_w = part(A2 + NWT * P, NWT * P).bitcast(I32).rearrange("p (t c) -> p t c", t=NWT)
        rel_w = part(A2, NWT * P).rearrange("p (t c) -> p t c", t=NWT)
        low_w = part(A2 + NWT * P, NWT * P).rearrange("p (t c) -> p t c", t=NWT)
        hi_w = part(0, NWT * P).bitcast(I32).rearrange("p (t c) -> p t c", t=NWT)
        padlist = part(A2, NSLOT // P * 4).bitcast(I32).rearrange("p (r c) -> p r c", c=4)
        A3 = A2 + NSLOT // P * 4
        PADS = EPAD - E
        padends = work[0:1, A3:A3 + 2 * PADS].bitcast(I32).rearrange("p (m c) -> p m c", m=2)
        assert A5 + 2 * P + NWT <= A2 and A1 + 4 * P + 3 * P // 2 <= A2 and A3 + 2 * PADS <= AW and 2 * (HB1 + HB2) + EW // 2 <= OHW and NWT * P <= A2
        piece = [part(s * BLK7 * D, BLK7 * D).rearrange("p (b d) -> p b d", b=BLK7) for s in range(2)]
        slow_sums = part(0, NB * D).rearrange("p (b d) -> p b d", b=NB)
        slow_rows = part(AW, SC * D).rearrange("p (c d) -> p c d", c=SC)
        slow_hot = part(AW + SC * D, SC * P).rearrange("p (c n) -> p c n", c=SC)
        assert SC * (D + P) <= OHW and 2 * BLK7 <= NB
        w1s = part(0, RING * K * H).rearrange("p (s k h) -> p s k h", s=RING, k=K)
        w2s = big[:, FB:FB + RING * HK * D].rearrange("p (s k d) -> p s k d", s=RING, k=HK)
        b2s = big[:, FB + RING * HK * D:FB + RING * (HK + 1) * D].rearrange("p (s d) -> p s d", s=RING)
        T0 = RING * K * H
        xg = part(T0, RING * D).rearrange("p (s d) -> p s d", s=RING)
        T1 = T0 + RING * D
        xT = part(T1, 2 * D).rearrange("p (s k n) -> p s k n", s=2, k=K)
        T2 = T1 + 2 * D
        h1 = part(T2, 2 * H).rearrange("p (s k n) -> p s k n", s=2, k=HK)
        T3 = T2 + 2 * H
        hs = part(T3, 2 * H).rearrange("p (s h) -> p s h", s=2)
        T4 = T3 + 2 * H
        yo = part(T4, RING * D).rearrange("p (s d) -> p s d", s=RING)
        T5 = T4 + RING * D
        b1_s = work[0:NEXP, T5:T5 + H]
        RW = BPG * 2 * D
        result_mem = ([part(g * RW, RW) for g in range(NFG // 2)] + [big[:, FB + g * RW:FB + (g + 1) * RW] for g in range(NFG // 2)]
                      + [part(NB * D, 2 * D)])
        results = [m.rearrange("p (b k d) -> p b k d", k=2, d=D) for m in result_mem]
        feats = part(0, NB * D).rearrange("p (b d) -> p b d", b=NB)
        assert T5 + H <= AW + OHW and T5 >= AW and (NB + 2) * D <= AW + OHW and NFG // 2 * RW <= NB * D and FB + RING * (HK + 1) * D <= NB * 2 * D

        NWIN = NWT * P
        edge = sb("edge", [P, NWIN])
        edge_lo = edge[:, 0:NWIN // 2].bitcast(BF16)
        edge_v = edge[:, NWIN // 2:NWIN].bitcast(BF16)
        src_lo = sb("src_lo", [P, NHG, HC], BF16)
        src_hi = part(AW + 2 * (HB1 + HB2), EW // 2).bitcast(BF16).rearrange("p (g c) -> p g c", g=NHG)
        ended = edge[0:NEXP, 0:192]
        tile_f = edge[0:1, 192:192 + 4 * 192].rearrange("p (r t) -> p r t", r=4)
        tile_i = edge[0:1, 960:960 + 2 * 192].bitcast(I32).rearrange("p (r t) -> p r t", r=2)

        iota_lo = sb("iota_lo", [P, P, WB], BF16)
        iota_v = sb("iota_v", [P, WV, WB], BF16)
        iota_i = sb("iota_i", [P, 128], I32)
        pcol_i = sb("pcol_i", [P, 1], I32)
        win_i = sb("win_i", [P, NWT], I32)
        iota = sb("iota", [P, 192])
        pcol = sb("pcol", [P, 1])
        pcols = sb("pcols", [P, 4])
        ident = sb("ident", [P, P])
        onesf = sb("onesf", [P, P])
        zeros = sb("zeros", [P, D])
        tri_b = sb("tri_b", [P, P], BF16)
        tri_eq = sb("tri_eq", [P, P])
        ones_b = sb("ones_b", [P, P], BF16)
        first_w = sb("first_w", [P, NWT])
        below = sb("below", [P, 3, NWT])
        signs = sb("signs", [P, 5, NWT])
        row_w = sb("row_w", [P, NWT], I32)
        edge_w = sb("edge_w", [P, NWT], I32)
        deg_w = sb("deg_w", [P, WN, NWT])
        held = sb("held", [P, 1])
        general_f = sb("general_f", [1, 1])
        general = sb("general", [1, 1], I32)

        Wg_s = sb("Wg_s", [P, K, NEXP])
        bg_s = sb("bg_s", [P, NEXP])
        gb_s = sb("gb_s", [P, 2, D])
        b1T = sb("b1T", [P, HK, NEXP])

        degs = sb("degs", [P, 2, NB])
        rs_out = sb("rs_out", [P, NB])
        rs_in = sb("rs_in", [P, 2 * NWT])
        pair_mem = sb("pair_mem", [P, 4 * D])
        pair_x = [pair_mem[:, s * 2 * D:(s + 1) * 2 * D].rearrange("p (b d) -> p b d", b=2) for s in range(2)]
        fblk = pair_mem[:, 0:D]
        bias_x = pair_mem[:, 2 * D:4 * D].rearrange("p (m d) -> p m d", m=2)
        mean, scale = pair_mem[:, 0:D], pair_mem[:, D:2 * D]
        res_mem = sb("res_mem", [P, 4 * D])
        res_buf = [res_mem[:, s * 2 * D:(s + 1) * 2 * D].rearrange("p (b d) -> p b d", b=2) for s in range(2)]
        Wx_s = res_mem[:, :].rearrange("p (k m d) -> p k m d", k=K, m=2)
        xTp = sb("xTp", [P, 2, K, P])
        fT = [xTp[:, s] for s in range(2)]
        picks = sb("picks", [P, 2, 2, 2, NEXP])
        ranked = sb("ranked", [P, 2, 2, NEXP])

        logit = sb("logit", [P, 2, NEXP])
        top8 = sb("top8", [P, 2, 8])
        top8i = sb("top8i", [P, 2, 8], U32)
        expert = sb("expert", [P, 2, 2, 2])
        both = sb("both", [P, 2, 2, NEXP], BF16)
        before = sb("before", [P, 2, NEXP], BF16)
        gap = sb("gap", [P, 2, 2])
        egap = sb("egap", [P, 2, 2])
        rank = sb("rank", [P, 2, 2])
        over = sb("over", [P, 2, 2])
        slot_f = sb("slot_f", [P, 2, 2])
        slot = sb("slot", [P, 2, 2, 2], I32)
        entry = sb("entry", [P, 2, 2, 2, 4], I32)
        tok_i = sb("tok_i", [P, NB, 2, 2], I32)

        cntc = sb("cntc", [NEXP, 8])
        cnti = sb("cnti", [NEXP, 2], I32)
        last_i = sb("last_i", [1, 1], I32)

        lt = sb("lt", [P, RING, 4], I32)

        slow_src = sb("slow_src", [P, SC], I32)
        slow_dst = sb("slow_dst", [P, SC], I32)
        slow_rel = sb("slow_rel", [P, SC])

        stats = sb("stats", [P, BPG, 6])
        moments = sb("moments", [P, 2, BPG, 2])
        inv = sb("inv", [P, 2, BPG])
        shift = sb("shift", [P, 2, BPG])
        eps_c = sb("eps_c", [P, 1])

        banks = ctx.enter_context(nc.psum_tensor("banks", [P, 8, 512], F32))
        bank = [banks[:, i, :] for i in range(8)]
        hist_ps = bank[0][:, 0:NB]
        prod_ps = [bank[1], bank[2]]
        fT_ps = bank[3][:, 0:K * P].rearrange("p (k n) -> p k n", k=K)
        bins_ps, bin_ps, below_ps = bank[4][:, 0:NWT], bank[5][0:NWT, 0:1], bank[6][:, 0:NWT]
        small = bank[4]
        turned_ps = [bank[6 + m].rearrange("p (t n) -> p t n", t=4) for m in range(2)]
        built_ps = [banks[:, 2 * s:2 * s + 2, :] for s in range(2)]
        agg_ps = [bank[4], bank[5]]
        slow_ps = bank[5]
        xT_ps = bank[6].rearrange("p (b k n) -> p b k n", b=2, k=K)
        logit_ps = bank[7][:, 0:2 * NEXP].rearrange("p (b e) -> p b e", b=2)
        rank_ps = bank[7][:, 2 * NEXP:4 * NEXP].rearrange("p (b e) -> p b e", b=2)
        tx_ps = [bank[i][:, 0:K * P].rearrange("p (k n) -> p k n", k=K) for i in (0, 1)]
        h_ps = [bank[i] for i in (2, 3)]
        hT_ps = [bank[i].rearrange("p (k n) -> p k n", k=HK) for i in (6, 7)]
        y_ps = [bank[i][:, 0:D] for i in (4, 5)]
        sum_ps, sq_ps = bank[6][:, 0:D], bank[7][:, 0:D]

        src_in, feats_first, feats_in, weights_in, bases_in, pads_out = sem("src_in"), sem("feats_first"), sem("feats_in"), sem("weights_in"), sem("bases_in"), sem("pads_out")
        tails_set, lists_set, lists_out, y_zeroed = sem("tails_set"), sem("lists_set"), sem("lists_out"), sem("y_zeroed")
        iotas, consts, b1_in = sem("iotas"), sem("consts"), sem("b1_in")
        hist_ready, hist_used, hist_done = sem("hist_ready"), sem("hist_used"), sem("hist_done")
        deg_clipped, deg_root, rs_ready = sem("deg_clipped"), sem("deg_root"), sem("rs_ready")
        f_staged, fT_summed, fT_ready = sem("f_staged"), sem("fT_summed"), sem("fT_ready")
        bias_ready, multiplied, prod_copied, biased = sem("bias_ready"), sem("multiplied"), sem("prod_copied"), sem("biased")
        res_out = [sem("res_out0"), sem("res_out1")]
        upper_ready, split = sem("upper_ready"), sem("split")
        bases_set, bases_hot, binned, bins_copied, bins_summed, sums_copied, rows_counted, row_ready = (
            sem("bases_set"), sem("bases_hot"), sem("binned"), sem("bins_copied"), sem("bins_summed"), sem("sums_copied"), sem("rows_counted"), sem("row_ready"))
        found_in, found_counted, edge_ready = sem("found_in"), sem("found_counted"), sem("edge_ready")
        dst_w_in, src_w_in, window_counted = sem("dst_w_in"), sem("src_w_in"), sem("window_counted")
        digits_ready, digits_turned, edges_ready = sem("digits_ready"), sem("digits_turned"), sem("edges_ready")
        deg_ready, deg_placed, general_ready, blocks_ready = sem("deg_ready"), sem("deg_placed"), sem("general_ready"), sem("blocks_ready")
        piece_ready, piece_out = sem("piece_ready"), [sem("piece_out0"), sem("piece_out1")]
        slow_edges_in, slow_rows_in, slow_hot_ready, slow_summed, slow_used = (
            sem("slow_edges_in"), sem("slow_rows_in"), sem("slow_hot_ready"), sem("slow_summed"), sem("slow_used"))
        slow_res_in, slow_added, slow_res_out = sem("slow_res_in"), sem("slow_added"), sem("slow_res_out")
        onehot_ready, built, evacuated, summed, x_made, res_in = (
            sem("onehot_ready"), sem("built"), sem("evacuated"), sem("summed"), sem("x_made"), [sem("res_in0"), sem("res_in1")])
        x_turned, xT_ready = sem("x_turned"), sem("xT_ready")
        logits_done, both_ready, gap_ready, egap_ready = sem("logits_done"), sem("both_ready"), sem("gap_ready"), sem("egap_ready")
        ranks_done, slots_ready = sem("ranks_done"), sem("slots_ready")
        list_out = [sem("list_out0"), sem("list_out1")]
        x_out = [sem("x_out0"), sem("x_out1")]
        x_in = sem("x_in")
        tables, tables_col, tiles_ready, b1_turned, b1_ready = (
            sem("tables"), sem("tables_col"), sem("tiles_ready"), sem("b1_turned"), sem("b1_ready"))
        list_in = [sem(f"list_in{s}") for s in range(RING)]
        y_out = [sem(f"y_out{s}") for s in range(RING)]
        xg_in = [sem(f"xg_in{s}") for s in range(RING)]
        w_in = [sem(f"w_in{s}") for s in range(RING)]
        tx_done, tx_ready, h_done, hs_ready, hT_done, h1_ready, tile_done, y_ready = (
            sem("tx_done"), sem("tx_ready"), sem("h_done"), sem("hs_ready"), sem("hT_done"), sem("h1_ready"), sem("tile_done"), sem("y_ready"))
        y_in, f_in = [sem(f"y_in{g}") for g in range(NFG + 1)], [sem(f"f_in{m}") for m in range(-(-(NFG + 1) // 3))]
        y_summed, sum_done = sem("y_summed"), sem("sum_done")
        centred, squared, sq_halved, sq_done = sem("centred"), sem("squared"), sem("sq_halved"), sem("sq_done")
        root_ready, var_ready, f_ready, scale_ready, scaled = sem("root_ready"), sem("var_ready"), sem("f_ready"), sem("scale_ready"), sem("scaled")
        lnvar_ready, lnroot_ready, shift_ready, out_ready, out_done = (
            sem("lnvar_ready"), sem("lnroot_ready"), sem("shift_ready"), sem("out_ready"), sem("out_done"))

        block = ctx.enter_context(nc.Block())

        def x_out_total(parity):
            return 16 * sum(j % 2 == parity for j in range(NPAIR + 1))

        def res_out_total(m):
            return 16 * sum(j // LATE == m for j in range(NPC))

        def list_out_total(parity):
            return sum(2 * (2 if j < NPAIR else 1) for j in range(NPAIR + 1) if j % 2 == parity)

        def blocks(a, b0, n):
            return a[b0 * P:(b0 + n) * P, :].rearrange("(b p) d -> p b d", p=P)

        def blocks_of(j):
            return 1 if isinstance(j, int) and j == NPAIR else 2

        def rows_of(j):
            return TAIL if isinstance(j, int) and j == NPAIR else P

        def fifth(q):
            return range(-(-q * NB // 5), -(-(q + 1) * NB // 5))

        whole, rest = divmod(NROW - 1, RC)

        def group(g):
            return (P, slice(g * BPG, (g + 1) * BPG)) if g < NFG else (TAIL, slice(NB - 1, NB))

        def group_of(a, g):
            return blocks(a, g * BPG, BPG) if g < NFG else a[(NB - 1) * P:N, :].unsqueeze(1)

        NW = 16 * 8
        B_FOUND, B_WINDOW = (10, 6), (26, 14)
        G_EDGE, G_DIGITS, G_DEG = 21, 43, 46
        B_DIGITS = 46
        NTG = -(-NWT // 4)
        assert (G_DIGITS - LEAD) % 2 == 0 and G_DIGITS + NTG <= NHG // 2 and NB - B_DIGITS <= NHG // 2 - G_DIGITS and sum(B_WINDOW) <= G_DIGITS - LEAD <= B_DIGITS

        @block.sync
        def _(sp):
            sp.dma_start(src_i[:, 0:EC], src[0:EC * P].rearrange("(p c) -> p c", p=P)).then_inc(src_in, 16)
            sp.wait_ge(bases_set, 1)
            sp.dma_start(bases_i[0:whole, 0, :], dst[0:whole * RC * ROW].rearrange("(p c e) -> p c e", c=RC, e=ROW)[:, :, 0],
                         allow_slow_non_contiguous=True).then_inc(bases_in, 16)
            for c in range(rest + 1):
                at = (whole * RC + c) * ROW
                sp.dma_start(bases_i[whole:whole + 1, 0, c:c + 1], dst[at:at + 1].rearrange("(p c) -> p c", p=1)).then_inc(bases_in, 16)
            sp.wait_ge(tails_set, 1)
            sp.dma_start(src_i[0:EREST, EC:EC + 1], src[EC * P:E].rearrange("(p c) -> p c", c=1)).then_inc(src_in, 16)
            sp.dma_start(G[:, 0:FIRST, D:2 * D], blocks(x, 0, FIRST)).then_inc(feats_first, 16)
            for m, (a, flat) in enumerate(((dst, dst_flat), (src, src_flat))):
                sp.dma_start(flat[0:EC * P].rearrange("(p c) -> p c", p=P), a[0:EC * P].rearrange("(p c) -> p c", p=P)).then_inc(pads_out, 16)
                sp.dma_start(flat[EC * P:E].rearrange("(p c) -> p c", p=1), a[EC * P:E].rearrange("(p c) -> p c", p=1)).then_inc(pads_out, 16)
                sp.dma_start(flat[E:EPAD].rearrange("(p c) -> p c", p=1), padends[:, m, :]).then_inc(pads_out, 16)
            sp.dma_start(G[:, FIRST:NB - 1, D:2 * D], blocks(x, FIRST, NB - 1 - FIRST)).then_inc(feats_in, 16)
            sp.dma_start(G[0:TAIL, NB - 1, D:2 * D], x[(NB - 1) * P:N, :]).then_inc(feats_in, 16)
            sp.wait_ge(lists_set, 1)
            sp.dma_start(lists.rearrange("(p r) c -> p (r c)", p=P), padlist[:, :, :].rearrange("p r c -> p (r c)")).then_inc(lists_out, 16)
            for j in range(NPC):
                sp.wait_ge(biased, j + 1)
                sp.dma_start(blocks(restab, j * BLK7, BLK7), G[:, j * BLK7:(j + 1) * BLK7, D:2 * D]).then_inc(res_out[j // LATE], 16)
            for m in range(2):
                sp.wait_ge(res_out[m], res_out_total(m))
            sp.wait_ge(consts, 1)
            n = N * 2 // P
            sp.dma_start(ytab[0:n * P, :].rearrange("(p r) d -> p r d", p=P),
                         zeros[:, :].unsqueeze(1).to_broadcast([P, n, D])).then_inc(y_zeroed, 16)
            sp.dma_start(ytab[n * P:2 * N, :], zeros[0:2 * N - n * P, :]).then_inc(y_zeroed, 16)
            sp.wait_ge(general_ready, 1)
            is_general = sp.value_load(general[0:1, 0:1], min_val=0, max_val=1)
            with sp.If(is_general > 0):
                for j in range(NPC):
                    sp.wait_ge(piece_ready, j + 1)
                    sp.dma_start(blocks(htab, j * BLK7, BLK7), piece[j % 2]).then_inc(piece_out[j % 2], 16)
                with sp.Fori(0, NSG) as g:
                    sp.wait_ge(slow_used, g + 1)
                    sp.dma_start(slow_src[:, :], src_flat[ds(g * (P * SC), P * SC)].rearrange("(p c) -> p c", p=P)).then_inc(slow_edges_in, 16)
                    sp.dma_start(slow_dst[:, :], dst_flat[ds(g * (P * SC), P * SC)].rearrange("(p c) -> p c", p=P)).then_inc(slow_edges_in, 16)
                with sp.Fori(0, NB) as b:
                    sp.dma_start(fblk, restab[ds(b * P, P), :]).then_inc(slow_res_in, 16)
                    sp.wait_ge(slow_added, b + 1)
                    sp.dma_start(restab[ds(b * P, P), :], fblk).then_inc(slow_res_out, 16)
                    stored = sp.to_reg(b * 16 + 16)
                    sp.wait_ge(general_ready, 1)
                    sp.wait_ge(slow_res_out, stored)

            def load_res(j, s, nb):
                sp.dma_start(res_buf[s][:, 0:nb, :], restab[ds(j * (2 * P), nb * P), :].rearrange("(b p) d -> p b d", p=P)).then_inc(res_in[s], 16)

            def store_x(j, s, nb):
                sp.wait_ge(x_made, j * 2 + (nb + 2))
                sp.dma_start(xtab[ds(j * (2 * P), nb * P), :].rearrange("(b p) d -> p b d", p=P), pair_x[s][:, 0:nb, :]).then_inc(x_out[s], 16)

            sp.wait_ge(prod_copied, NB + 2)
            for s in range(2):
                load_res(s, s, 2)
            with sp.Fori(0, NPAIR // 2 - 1) as i:
                for s in range(2):
                    store_x(i * 2 + s, s, 2)
                    load_res(i * 2 + (s + 2), s, 2)
            store_x(NPAIR - 2, 0, 2)
            load_res(NPAIR, 0, 1)
            store_x(NPAIR - 1, 1, 2)
            store_x(NPAIR, 0, 1)
            for s in range(2):
                sp.wait_ge(x_out[s], x_out_total(s))
            sp.wait_ge(tiles_ready, 1)
            for s in range(2):
                sp.wait_ge(list_out[s], 16 * list_out_total(s))
            last = sp.value_load(last_i[0:1, 0:1], min_val=1, max_val=TMAX)
            with sp.Fori(0, TLOOP // RING) as i:
                with sp.If(i * RING < last + 1):
                    for s in range(RING):
                        t = i * RING + s
                        with sp.If(t < last + 1):
                            code = sp.value_load(tile_i[0:1, 0, ds(t, 1)], min_val=0, max_val=(8 * NEXP * RING) - 1)
                            e = sp.snap((code >> CE) & (NEXP - 1))
                            j = sp.snap((code >> CJ) & (CAP // P - 1))
                            ws = sp.snap(code & (RING - 1))
                            sent, used, at = sp.to_reg(i * 16 + 16), sp.to_reg(t + 1), sp.snap(e * LROWS + j * P)
                            sp.wait_ge(tiles_ready, 1)
                            sp.wait_ge(y_out[s], sent)
                            sp.wait_ge(tile_done, used)
                            sp.dma_start(lt[:, s, :], lists[ds(at, P), :]).then_inc(list_in[s], 16)
                            with sp.If(j == 0):
                                sp.dma_start(w1s[:, ds(ws, 1), :, :].rearrange("p s k h -> p (s k) h"),
                                             w1[ds(e, 1), :, :].rearrange("e (k p) h -> p (e k) h", p=P)).then_inc(w_in[s], 16)
                                sp.dma_start(w2s[:, ds(ws, 1), :, :].rearrange("p s k d -> p (s k) d"),
                                             w2[ds(e, 1), :, :].rearrange("e (k p) d -> p (e k) d", p=P)).then_inc(w_in[s], 16)
                                sp.dma_start(b2s[:, ds(ws, 1), :].rearrange("p s d -> p (s d)"),
                                             b2[ds(e, 1), :].to_broadcast([P, D])).then_inc(w_in[s], 16)
                            with sp.Else():
                                sp.sem_inc(w_in[s], 48)
                for h, pieces in enumerate((range(0, NPC // 2), range(NPC // 2, NPC))):
                    with sp.If(i == h + 1):
                        for j in pieces:
                            sp.dma_start(F[:, j * BLK7:(j + 1) * BLK7, :], blocks(xtab, j * BLK7, BLK7)).then_inc(x_in, 16)
            n_tiles = sp.snap(last)
            for s in range(RING):
                sent = sp.to_reg(((n_tiles + (RING - 1 - s)) // RING) * 16 + 16)
                sp.wait_ge(tiles_ready, 1)
                sp.wait_ge(y_out[s], sent)
            pairs = ytab[0:2 * N, :].rearrange("(n k) d -> n (k d)", k=2)
            for g in range(NFG + 1):
                q, b = group(g)
                sp.dma_start(results[g][0:q].rearrange("p b k d -> p b (k d)"), group_of(pairs, g)).then_inc(y_in[g], 16)
            for g in range(NFG + 1):
                q, b = group(g)
                if g < NFG:
                    sp.wait_ge(y_summed, g // 2 + 1)
                sp.dma_start(feats[0:q, b], group_of(x, g)).then_inc(f_in[g // 3], 16)
            for g in range(NFG + 1):
                q, b = group(g)
                sp.wait_ge(out_ready, g + 1)
                sp.dma_start(group_of(out, g), F[0:q, b, :]).then_inc(out_done, 16)
            sp.wait_ge(out_done, 16 * (NFG + 1))

        @block.gpsimd
        def _(pool):
            pool.iota(iota_i[:, :], [[1, 128]], base=0, channel_multiplier=0)
            pool.iota(win_i[:, :], [[WN * P, NWT]], base=0, channel_multiplier=WN)
            pool.iota(pcol_i[:, :], [[0, 1]], base=0, channel_multiplier=1).then_inc(iotas, 1)
            pool.memset(padlist[:, :, 0], N)
            pool.memset(padlist[:, :, 1], 2 * N)
            pool.memset(padlist[:, :, 2:4], 0).then_inc(lists_set, 1)
            pool.iota(tok_i[:, :, :, 0], [[P, NB], [0, 2]], base=0, channel_multiplier=1)
            pool.iota(tok_i[:, :, :, 1], [[2 * P, NB], [1, 2]], base=0, channel_multiplier=2).then_inc(iotas, 1)

            def add_bias(j):
                at = G[:, j * BLK7:(j + 1) * BLK7, D:2 * D]
                pool.wait_ge(bias_ready, 1)
                pool.wait_ge(prod_copied, (j + 1) * BLK7 + 2)
                pool.tensor_tensor(at, at, bias_x[:, 0, :].unsqueeze(1).to_broadcast([P, BLK7, D]), ALU.add).then_inc(biased, 1)

            pool.wait_ge(pads_out, 16 * 6)
            pool.wait_ge(lists_out, 16)
            pool.wait_ge(row_ready, 1)
            for t in range(NWT):
                pool.indirect_dma_start(found[:, t, :], None, dstpad, bass.IndirectOffsetOnAxis(ap=row_w[:, t:t + 1], axis=0)).then_inc(found_in, 16)
            add_bias(0)
            pool.wait_ge(edge_ready, 1)
            for ends, flat, done in ((dst_w, dst_flat, dst_w_in), (src_w, src_flat, src_w_in)):
                for t in range(NWT):
                    pool.indirect_dma_start(ends[:, t, :], None, flat.rearrange("(n o) -> n o", o=1),
                                            bass.IndirectOffsetOnAxis(ap=edge_w[:, t:t + 1], axis=0)).then_inc(done, 16)
            for j in range(1, NPC):
                add_bias(j)

            pool.wait_ge(general_ready, 1)
            is_general = pool.value_load(general[0:1, 0:1], min_val=0, max_val=1)
            with pool.If(is_general > 0):
                for s in range(2):
                    pool.wait_ge(piece_out[s], 16 * sum(j % 2 == s for j in range(NPC)))
                with pool.Fori(0, NSG) as g:
                    loaded = pool.to_reg(g * 32 + 32)
                    pool.wait_ge(general_ready, 1)
                    pool.wait_ge(slow_edges_in, loaded)
                    for c in range(SC):
                        pool.indirect_dma_start(slow_rows[:, c, :], None, htab, bass.IndirectOffsetOnAxis(ap=slow_src[:, c:c + 1], axis=0)
                                                ).then_inc(slow_rows_in, 16)

            pool.wait_ge(y_zeroed, 32)
            for s in range(RING):
                pool.dma_start(ytab[2 * N + s:2 * N + s + 1, :], zeros[0:1, :]).then_inc(y_out[s], 16)

            def send(j, s, nb, valid):
                placed = pool.to_reg(j + 1)
                pool.wait_ge(lists_out, 16)
                pool.wait_ge(slots_ready, placed)
                for b in range(nb):
                    for k in range(2):
                        pool.indirect_dma_start(lists, bass.IndirectOffsetOnAxis(ap=slot[0:valid, s, b, k:k + 1], axis=0),
                                                entry[0:valid, s, b, k, :], None, bounds_check=NSLOT - 1, oob_is_err=False
                                                ).then_inc(list_out[s], 16)

            with pool.Fori(0, NPAIR // 2) as i:
                for s in range(2):
                    send(i * 2 + s, s, 2, P)
            send(NPAIR, NPAIR % 2, 1, TAIL)

            for s in range(2):
                pool.wait_ge(x_out[s], x_out_total(s))
            pool.wait_ge(tiles_ready, 1)
            last = pool.value_load(last_i[0:1, 0:1], min_val=1, max_val=TMAX)

            def fetch(t, i, s):
                with pool.If(t < last + 1):
                    listed, turned = pool.to_reg(i * 16 + 16), pool.to_reg(t + 1)
                    pool.wait_ge(tiles_ready, 1)
                    pool.wait_ge(list_in[s % RING], listed)
                    pool.wait_ge(tx_done, turned)
                    pool.indirect_dma_start(xg[:, s % RING, :], None, xtab, bass.IndirectOffsetOnAxis(ap=lt[:, s % RING, 0:1], axis=0)
                                            ).then_inc(xg_in[s % RING], 16)

            for t in range(AHEAD):
                fetch(t, 0, t)
            with pool.Fori(0, TLOOP // RING) as i:
                with pool.If(i * RING < last + 1):
                    for s in range(RING):
                        t = i * RING + s
                        with pool.If(t < last):
                            done = pool.to_reg(t + 3)
                            pool.wait_ge(tiles_ready, 1)
                            pool.wait_ge(y_ready, done)
                            pool.indirect_dma_start(ytab, bass.IndirectOffsetOnAxis(ap=lt[:, s, 1:2], axis=0), yo[:, s, :], None,
                                                    bounds_check=2 * N - 1, oob_is_err=False
                                                    ).then_inc(y_out[s], 16)
                        fetch(t + AHEAD, i + (s + AHEAD) // RING, s + AHEAD)

            for g in range(NFG + 1):
                q, b = group(g)
                v = feats[0:q, b]
                pool.wait_ge(f_in[g // 3], 16 * len(range(g // 3 * 3, min(g // 3 * 3 + 3, NFG + 1))))
                pool.tensor_tensor(v, v, gb_s[0:q, 1, :].unsqueeze(1).to_broadcast(list(v.shape)), ALU.add).then_inc(f_ready, 1)
            pool.wait_ge(scale_ready, 1)
            for g in range(1, NFG + 1):
                q, b = group(g)
                pool.tensor_tensor(F[0:q, b], F[0:q, b], scale[0:q, :].unsqueeze(1).to_broadcast(list(F[0:q, b].shape)), ALU.mult).then_inc(scaled, 1)

        @block.scalar
        def _(act):
            for m, w in enumerate((W_gc, W_res)):
                act.dma_start(Wx_s[:, :, m, :], w.rearrange("(k p) n -> p k n", p=P)).then_inc(weights_in, 16)
            act.dma_start(Wg_s[:, :, :], Wg.rearrange("(k p) n -> p k n", p=P)).then_inc(weights_in, 16)
            for tile, v in ((bias_x[:, 0, :], b_gc), (bias_x[:, 1, :], b_res), (bg_s[:, :], bg),
                            (gb_s[:, 0, :], gamma), (gb_s[:, 1, :], beta)):
                act.dma_start(tile, v.unsqueeze(0).to_broadcast([P, v.shape[0]])).then_inc(weights_in, 16)

            def count_below(signs_out, ends, threshold, total):
                nc.scalar.activation(signs_out, ends, ACT.Sign, bias=threshold, scale=-1.0, accum_out=total)

            nc.scalar.preload_act_table(ACT.Sign)

            def stage_feats(b):
                if not isinstance(b, int) or b > 0:
                    act.wait_ge(fT_summed, b)
                nc.scalar.copy(fblk, G[:, ds(b, 1), D:2 * D].rearrange("p b d -> p (b d)")).then_inc(f_staged, 1)

            def turn_feats(b, s):
                act.wait_ge(fT_summed, b + 1)
                nc.scalar.copy(fT[s], fT_ps).then_inc(fT_ready, 1)

            def copy_product(b, s):
                act.wait_ge(multiplied, b + 1)
                nc.scalar.copy(G[:, ds(b, 1), :].rearrange("p b d -> p (b d)"), prod_ps[s]).then_inc(prod_copied, 1)

            def feats_step(b, s):
                if not isinstance(b, int) or b > 0:
                    copy_product(b - 1, 1 - s)
                if not isinstance(b, int) or b + 1 < NB:
                    turn_feats(b + 1, 1 - s)
                if not isinstance(b, int) or b + 2 < NB:
                    stage_feats(b + 2)

            def share(b, first, n):
                return range((b - first) * NWT // n, (b - first + 1) * NWT // n)

            act.wait_ge(feats_first, 16)
            stage_feats(0)
            turn_feats(0, 0)
            stage_feats(1)
            for b in range(FIRST - 2):
                feats_step(b, b % 2)
            act.wait_ge(feats_in, 32)
            with act.Fori(FIRST // 2 - 1, B_FOUND[0] // 2) as i:
                for s in range(2):
                    feats_step(i * 2 + s, s)
            act.wait_ge(found_in, 16 * NWT)
            first, n = B_FOUND
            for b in range(first, first + n):
                feats_step(b, b % 2)
                for t in share(b, first, n):
                    count_below(found[:, t, :], found[:, t, :], below[:, 0, t:t + 1], signs[:, 1, t:t + 1])
            act.drain().then_inc(found_counted, 1)
            with act.Fori((first + n) // 2, B_WINDOW[0] // 2) as i:
                for s in range(2):
                    feats_step(i * 2 + s, s)
            act.wait_ge(dst_w_in, 16 * NWT)

            def count_window(t):
                tile = dst_w[:, ds(t, 1), :].rearrange("p t c -> p (t c)")
                act.drain()
                for m in range(3):
                    count_below(spare[:, m * P:(m + 1) * P], tile, below[:, m, ds(t, 1)], signs[:, 2 + m, ds(t, 1)])

            first, n = B_WINDOW
            for b in range(first, first + n):
                feats_step(b, b % 2)
                for t in share(b, first, n):
                    count_window(t)
            act.drain().then_inc(window_counted, 1)
            for b in range(first + n, B_DIGITS):
                feats_step(b, b % 2)

            for b in range(B_DIGITS, max(NB + 1, B_DIGITS + NTG)):
                if b < NB:
                    feats_step(b, b % 2)
                elif b == NB:
                    copy_product(NB - 1, (NB - 1) % 2)
                if b - B_DIGITS < NTG:
                    t = (b - B_DIGITS) * 4
                    n = min(4, NWT - t)
                    for m, v in enumerate((edge_lo, edge_v)):
                        act.wait_ge(digits_turned, 2 * (t // 4) + m + 1)
                        nc.scalar.copy(v[:, t * P:(t + n) * P].rearrange("p (t n) -> p t n", t=n), turned_ps[m][:, 0:n, :]).then_inc(edges_ready, 1)

            nc.scalar.preload_act_table(ACT.Sqrt)
            act.wait_ge(deg_clipped, 1)
            nc.scalar.activation(rs_in[:, :], rs_in[:, :], ACT.Sqrt).then_inc(deg_root, 1)
            act.wait_ge(general_ready, 1)
            is_general = act.value_load(general[0:1, 0:1], min_val=0, max_val=1)
            act.wait_ge(deg_clipped, 2)
            nc.scalar.activation(rs_out[:, :], degs[:, 0, :], ACT.Sqrt).then_inc(deg_root, 1)

            def upper_part(j):
                act.wait_ge(res_out[j // LATE], res_out_total(j // LATE))
                act.wait_ge(rs_ready, 1)
                for b in range(j * BLK7, (j + 1) * BLK7):
                    m = nc.scalar.activation(parts[:, b, D:2 * D], G[:, b, 0:D], ACT.Copy, scale=rs_out[:, b:b + 1])
                m.then_inc(upper_ready, 1)

            def evacuate(n, h, i):
                if i == 0:
                    act.wait_ge(summed, n + 1)
                act.wait_ge(general_ready, 1)
                act.wait_ge(built, n * BPB + (i + OHB + 1))
                nc.scalar.copy(counts[h][:, :, i * WB * WN:(i + 1) * WB * WN].rearrange("p b (h w) -> p h w b", h=2),
                               built_ps[i % 2][:, :, 0:WB * WV // 2].rearrange("p h (w b) -> p h w b", b=NB)).then_inc(evacuated, 1)

            def turn_x(j, nb):
                act.wait_ge(x_turned, j + 1)
                nc.scalar.copy(xTp[:, 0:nb], xT_ps[:, 0:nb]).then_inc(xT_ready, 1)

            def gate_exp(j, s, nb):
                act.wait_ge(gap_ready, j + 1)
                nc.scalar.activation(egap[:, s, 0:nb], gap[:, s, 0:nb], ACT.Exp).then_inc(egap_ready, 1)

            def step(j, s):
                before_it = not isinstance(j, int) or j > 0
                for h in range(2):
                    for i in range(BPB):
                        evacuate(j * 2 + (h + 1), 1 - h, i)
                        if (h, i) == (0, 1) and before_it:
                            turn_x(j - 1, 2)
                        if (h, i) == (1, 1) and before_it:
                            gate_exp(j - 1, 1 - s, 2)

            with act.If(is_general > 0):
                for j in range(NPC):
                    upper_part(j)
                act.wait_ge(deg_clipped, 3)
                nc.scalar.activation(rs_in[:, 0:NB], degs[:, 1, :], ACT.Sqrt).then_inc(deg_root, 1)
                for i in range(BPB):
                    evacuate(0, 0, i)
            with act.Else():
                for i in range(BPB):
                    evacuate(0, 0, i)
                    if i % 2 == 0:
                        upper_part(i // 2)
                for j in range(BPB // 2, NPC):
                    upper_part(j)
            nc.scalar.preload_act_table(ACT.Exp)
            for j in range(2):
                step(j, j)
            with act.Fori(1, NPAIR // 2) as i:
                for s in range(2):
                    step(i * 2 + s, s)
            turn_x(NPAIR - 1, 2)
            gate_exp(NPAIR - 1, (NPAIR - 1) % 2, 2)
            turn_x(NPAIR, 1)
            gate_exp(NPAIR, NPAIR % 2, 1)

            act.dma_start(b1_s, b1).then_inc(b1_in, 16)
            act.wait_ge(b1_turned, 1)
            nc.scalar.copy(b1T[:, :, :], bank[7][:, 0:HK * NEXP].rearrange("p (k e) -> p k e", k=HK)).then_inc(b1_ready, 1)
            act.wait_ge(tiles_ready, 1)
            act.drain()
            last = act.value_load(last_i[0:1, 0:1], min_val=1, max_val=TMAX)
            nc.scalar.preload_act_table(ACT.Gelu)

            def turned(t, s):
                act.wait_ge(h_done, t + 1)
                act.wait_ge(tx_done, t + (RING + 1))
                nc.scalar.copy(xT[:, s % 2], tx_ps[s % 2]).then_inc(tx_ready, 1)

            def gelu(t, s):
                code = act.value_load(tile_i[0:1, 0, ds(t, 1)], min_val=0, max_val=(8 * NEXP * RING) - 1)
                e = act.snap((code >> CE) & (NEXP - 1))
                act.wait_ge(tile_done, t + (RING - 1))
                act.wait_ge(b1_ready, 1)
                act.wait_ge(hT_done, t + 3)
                for k in range(HK):
                    nc.scalar.activation(h1[:, s % 2, k, :], hT_ps[s % 2][:, k, :], ACT.Gelu,
                                         bias=b1T[:, k, ds(e, 1)]).then_inc(h1_ready, 1)

            turned(0, 0)
            turned(1, 1)
            with act.Fori(0, TLOOP // RING) as i:
                with act.If(i * RING < last + 1):
                    for s in range(1, RING + 1):
                        t = i * RING + s
                        with act.If(t < last):
                            turned(t + 1, s + 1)
                            gelu(t - 1, s - 1)
                        with act.Else():
                            with act.If(t < last + 1):
                                gelu(t - 1, s - 1)

            nc.scalar.preload_act_table(ACT.Sqrt)
            for g in range(NFG + 1):
                q, b = group(g)
                act.wait_ge(centred, g + 1)
                nc.scalar.activation(squares[0:q, b], F[0:q, b], ACT.Square).then_inc(squared, 1)
            act.wait_ge(var_ready, 1)
            nc.scalar.activation(scale[:, :], mean[:, :], ACT.Sqrt, bias=eps_c[:, :]).then_inc(root_ready, 1)

            def normalise(g):
                q, b = group(g)
                act.wait_ge(shift_ready, g + 1)
                for i in range(b.start, b.stop):
                    at = F[0:q, i, :]
                    m = nc.scalar.activation(at, at, ACT.Identity, bias=shift[0:q, g % 2, i - b.start:i - b.start + 1],
                                             scale=inv[0:q, g % 2, i - b.start:i - b.start + 1])
                m.then_inc(out_ready, 1)

            for g in range(NFG + 1):
                q, b = group(g)
                n = b.stop - b.start
                act.wait_ge(lnvar_ready, g + 1)
                nc.scalar.activation(inv[0:q, g % 2, 0:n], moments[0:q, g % 2, 0:n, 1], ACT.Sqrt, bias=eps_c[0:q, :]).then_inc(lnroot_ready, 1)
                if g > 0:
                    normalise(g - 1)
            normalise(NFG)

        @block.tensor
        def _(pe):
            pe.wait_ge(consts, 1)
            pe.sem_inc(hist_used, 2)
            pe.sem_inc(built, OHB)
            pe.sem_inc(summed, 2)
            pe.sem_inc(tx_done, RING)
            pe.sem_inc(tile_done, RING)
            pe.sem_inc(h_done, 2)
            pe.sem_inc(hT_done, 2)

            pe.wait_ge(bases_hot, 1)
            for c in range(RC):
                last = pe.matmul(bins_ps, base_lo[:, c, :], base_hi[:, c, :], start=(c == 0), stop=(c == RC - 1))
            last.then_inc(binned, 1)
            pe.wait_ge(bins_copied, 1)
            pe.matmul(bin_ps, bins, onesf[:, 0:1], start=True, stop=True).then_inc(bins_summed, 1)
            pe.matmul(below_ps, tri, bins, start=True, stop=False)
            pe.wait_ge(sums_copied, 1)
            pe.matmul(below_ps, bin_sums, tri[0:NWT, 0:NWT], start=False, stop=True).then_inc(rows_counted, 1)

            def count(g, s):
                pe.wait_ge(hist_ready, g + 1)
                for c in range(HC):
                    last = pe.matmul(hist_ps, hist_lo[s][:, :, c], hist_hi[s][:, :, c], start=False, stop=False, skip_group_check=True)
                last.then_inc(hist_used, 1)

            def turn_feats(b):
                if not isinstance(b, int) or b > 0:
                    pe.wait_ge(weights_in, NW)
                    pe.wait_ge(fT_ready, b)
                pe.wait_ge(weights_in, NW)
                pe.wait_ge(f_staged, b + 1)
                for k in range(K):
                    m = pe.transpose(fT_ps[:, k, :], fblk[:, k * P:(k + 1) * P], ident[:, :])
                m.then_inc(fT_summed, 1)

            def multiply(b, s):
                pe.wait_ge(fT_ready, b + 1)
                pe.wait_ge(prod_copied, b + 1)
                for m in range(2):
                    for k in range(K):
                        last = pe.matmul(prod_ps[s][:, m * D:(m + 1) * D], fT[s][:, k, :], Wx_s[:, k, m, :], start=(k == 0), stop=(k == K - 1))
                last.then_inc(multiplied, 1)

            def feats_step(b, s, pair=None):
                if not isinstance(b, int) or b + 1 < NB:
                    turn_feats(b + 1)
                if pair is not None:
                    count(pair * 2, 0)
                multiply(b, s)
                if pair is not None:
                    count(pair * 2 + 1, 1)

            def turn_digits(t):
                pe.wait_ge(digits_ready, 1)
                for m, v in enumerate((low_w, rel_w)):
                    if t > 0:
                        pe.wait_ge(edges_ready, 2 * (t // 4 - 1) + m + 1)
                    for q in range(min(4, NWT - t)):
                        last = pe.transpose(turned_ps[m][:, q, :], v[:, t + q, :], ident[:, :])
                    last.then_inc(digits_turned, 1)

            def place_degrees():
                pe.wait_ge(deg_ready, 1)
                for h in range(2):
                    for s in range(WN):
                        pe.matmul(small[:, h * 32:h * 32 + NWT], pick[:, h * WN + s, :], deg_w[:, s, :], start=(s == 0), stop=(s == WN - 1))
                pe.matmul(small[0:1, 64:65], held[:, :], onesf[:, 0:1], start=True, stop=True).then_inc(deg_placed, 1)

            pe.matmul(hist_ps, zeros[:, 0:P], zeros[:, 0:NB], start=True, stop=False, skip_group_check=True)
            with pe.Fori(0, LEAD) as i:
                for s in range(2):
                    count(i * 2 + s, s)
            pe.wait_ge(weights_in, NW)
            turn_feats(0)
            with pe.Fori(0, (G_DIGITS - LEAD) // 2) as i:
                for s in range(2):
                    feats_step(i * 2 + s, s, i * 2 + (s + LEAD))
            for b in range(G_DIGITS - LEAD, B_DIGITS):
                feats_step(b, b % 2)
            for i in range(NHG // 2 - G_DIGITS):
                b, pair = B_DIGITS + i, G_DIGITS + i
                if b < NB:
                    feats_step(b, b % 2, pair)
                else:
                    for s in range(2):
                        count(pair * 2 + s, s)
                if i < NTG:
                    turn_digits(i * 4)
                if i == 0:
                    place_degrees()
            count(NHG - 1, 0)
            pe.matmul(hist_ps, zeros[:, 0:P], zeros[:, 0:NB], start=False, stop=True, skip_group_check=True).then_inc(hist_done, 1)

            pe.wait_ge(general_ready, 1)
            is_general = pe.value_load(general[0:1, 0:1], min_val=0, max_val=1)
            with pe.If(is_general > 0):
                with pe.Fori(0, NSG) as g:
                    gathered = pe.to_reg(g * (16 * SC) + 16 * SC)
                    pe.wait_ge(general_ready, 1)
                    pe.wait_ge(slow_rows_in, gathered)
                    with pe.Fori(0, NB) as b:
                        pe.wait_ge(general_ready, 1)
                        pe.wait_ge(slow_hot_ready, g * NB + (b + 1))
                        for c in range(SC):
                            pe.matmul(slow_ps[:, 0:D], slow_hot[:, c, :], slow_rows[:, c, :], start=(c == 0), stop=(c == SC - 1))
                        for c in range(SC):
                            last = pe.matmul(slow_ps[:, D:D + 1], slow_hot[:, c, :], onesf[:, 0:1], start=(c == 0), stop=(c == SC - 1))
                        last.then_inc(slow_summed, 1)

            def build(n, i):
                pe.wait_ge(general_ready, 1)
                pe.wait_ge(onehot_ready, n * BPB + (i + 1))
                pe.wait_ge(evacuated, n * BPB + (i + 1))
                for w in range(WB):
                    at = (w % 4) * WV
                    last = pe.matmul(built_ps[i % 2][:, w // 4, at:at + WV], oh_lo[i % OHB][:, :, w], oh_v[i % OHB][:, :, w], start=True, stop=True)
                last.then_inc(built, 1)

            def add_up(n, h, q):
                if q == 0:
                    pe.wait_ge(general_ready, 1)
                    pe.wait_ge(evacuated, n * BPB + (BPB + 2))
                    pe.wait_ge(x_made, n + 1)
                for b in fifth(q):
                    if isinstance(n, int) and n == 0 and (b == fifth(q)[0] or b % BLK7 == 0):
                        pe.wait_ge(split, b // BLK7 + 1)
                    last = pe.matmul(agg_ps[h], counts[h][:, b, :], parts[:, b, :], start=(b == 0), stop=(b == NB - 1))
                if q == 4:
                    last.then_inc(summed, 1)

            def turn_x(j, s, nb):
                pe.wait_ge(general_ready, 1)
                pe.wait_ge(x_made, j * 2 + (nb + 2))
                for b in range(nb):
                    for k in range(K):
                        m = pe.transpose(xT_ps[:, b, k, :], pair_x[s][:, b, k * P:(k + 1) * P], ident[:, :])
                m.then_inc(x_turned, 1)

            def score(j, nb):
                pe.wait_ge(general_ready, 1)
                if not isinstance(j, int) or j > 0:
                    pe.wait_ge(slots_ready, j)
                pe.wait_ge(xT_ready, j + 1)
                for b in range(nb):
                    for k in range(K):
                        m = pe.matmul(logit_ps[:, b, :], xTp[:, b, k, :], Wg_s[:, k, :], start=(k == 0), stop=(k == K - 1))
                m.then_inc(logits_done, 1)

            def ranks(j, s, nb, valid):
                pe.wait_ge(general_ready, 1)
                pe.wait_ge(both_ready, j + 1)
                for b in range(nb):
                    pe.matmul(rank_ps[0:valid, b, :], tri_b[0:valid, 0:valid], both[0:valid, s, b, :], start=True, stop=False)
                    if b == 1:
                        pe.matmul(rank_ps[0:valid, b, :], ones_b[:, 0:valid], both[:, s, 0, :], start=False, stop=False)
                    m = pe.matmul(rank_ps[0:valid, b, :], ones_b[:, 0:valid], before[:, s, :], start=False, stop=True)
                m.then_inc(ranks_done, 1)

            def step(j, s):
                before_it = not isinstance(j, int) or j > 0
                for h in range(2):
                    for q in range(5):
                        add_up(j * 2 + h, h, q)
                        for i in range(min(2 * q, BPB), min(2 * q + 2, BPB)):
                            build(j * 2 + (h + 1), i)
                        if before_it:
                            if (h, q) == (0, 0):
                                turn_x(j - 1, 1 - s, 2)
                            if (h, q) == (0, 1):
                                score(j - 1, 2)
                            if (h, q) == (1, 0):
                                ranks(j - 1, 1 - s, 2, P)

            pe.wait_ge(prod_copied, NB + 2)
            for i in range(BPB):
                build(0, i)
            for j in range(2):
                step(j, j)
            with pe.Fori(1, NPAIR // 2) as i:
                for s in range(2):
                    step(i * 2 + s, s)
            add_up(NB - 1, 0, 0)
            turn_x(NPAIR - 1, (NPAIR - 1) % 2, 2)
            add_up(NB - 1, 0, 1)
            score(NPAIR - 1, 2)
            for q in range(2, 5):
                add_up(NB - 1, 0, q)
            ranks(NPAIR - 1, (NPAIR - 1) % 2, 2, P)
            turn_x(NPAIR, NPAIR % 2, 1)
            score(NPAIR, 1)
            ranks(NPAIR, NPAIR % 2, 1, TAIL)

            pe.wait_ge(tables_col, 1)
            pe.matmul(small[0:NEXP, 0:1], before[:, (NPAIR + 1) % 2, :], ones_b[:, 0:1], start=True, stop=True).then_inc(tables, 1)
            pe.wait_ge(tables_col, 2)
            pe.matmul(bank[2][0:NEXP, 0:1], tri_eq[0:NEXP, 0:NEXP], cntc[:, 1:2], start=True, stop=True).then_inc(tables, 1)
            pe.wait_ge(tables_col, 3)
            pe.matmul(bank[2][0:1, 0:TMAX], onesf[0:NEXP, 0:1], ended[:, 0:TMAX], start=True, stop=True)
            pe.matmul(bank[3][0:1, 0:TMAX], cntc[:, 1:2], ended[:, 0:TMAX], start=True, stop=True)
            pe.matmul(bank[5][0:1, 0:TMAX], cntc[:, 3:4], ended[:, 0:TMAX], start=True, stop=True)
            pe.matmul(bank[6][0:1, 0:1], cntc[:, 1:2], onesf[0:NEXP, 0:1], start=True, stop=True).then_inc(tables, 1)

            pe.wait_ge(b1_in, 16)
            for k in range(HK):
                m = pe.transpose(bank[7][:, k * NEXP:(k + 1) * NEXP], b1_s[:, k * P:(k + 1) * P], ident[0:NEXP, 0:NEXP])
            m.then_inc(b1_turned, 1)
            pe.wait_ge(tiles_ready, 1)
            pe.wait_ge(b1_ready, 1)
            last = pe.value_load(last_i[0:1, 0:1], min_val=1, max_val=TMAX)

            def turn(t, i, s):
                pe.wait_ge(tiles_ready, 1)
                pe.wait_ge(xg_in[s % RING], i * 16 + 16)
                pe.wait_ge(tx_ready, t + 1)
                for k in range(K):
                    m = pe.transpose(tx_ps[s % 2][:, k, :], xg[:, s % RING, k * P:(k + 1) * P], ident[:, :])
                m.then_inc(tx_done, 1)

            def slots_of(t):
                return parts_of(pe.value_load(tile_i[0:1, 1, ds(t, 1)], min_val=0, max_val=RING * RING - 1))

            def parts_of(code):
                return pe.snap(code & (RING - 1)), pe.snap((code >> CE) & (RING - 1))

            def layer1(t, i, s, ws):
                pe.wait_ge(w_in[s % RING], i * 48 + 48)
                pe.wait_ge(hs_ready, t + 1)
                pe.wait_ge(tiles_ready, 1)
                pe.wait_ge(tx_ready, t + 3)
                for k in range(K):
                    m = pe.matmul(h_ps[s % 2][:, :], xT[:, s % 2, k, :], w1s[:, ds(ws, 1), k, :].rearrange("p s h -> p (s h)"),
                                  start=(k == 0), stop=(k == K - 1))
                m.then_inc(h_done, 1)

            def turn_h(t, s):
                pe.wait_ge(h1_ready, t * HK + HK)
                pe.wait_ge(tiles_ready, 1)
                pe.wait_ge(hs_ready, t + 3)
                for k in range(HK):
                    m = pe.transpose(hT_ps[s % 2][:, k, :], hs[:, s % 2, k * P:(k + 1) * P], ident[:, :])
                m.then_inc(hT_done, 1)

            def layer2(t, s, ws):
                pe.wait_ge(y_ready, t + 1)
                for k in range(HK):
                    pe.wait_ge(tiles_ready, 1)
                    pe.wait_ge(h1_ready, t * HK + (2 * HK + k + 1))
                    m = pe.matmul(y_ps[s % 2], h1[:, s % 2, k, :], w2s[:, ds(ws, 1), k, :].rearrange("p s d -> p (s d)"),
                                  start=(k == 0), stop=(k == HK - 1))
                m.then_inc(tile_done, 1)

            def tiles_from(i, s, slots):
                t = i * RING + s
                with pe.If(t < last):
                    ws, ws_before = slots or parts_of(pe.snap(next_code, min_val=0, max_val=RING * RING - 1))
                    turn(t + 1, i + (s + 1) // RING, (s + 1) % RING)
                    turn_h(t - 1, s - 1)
                    layer1(t, i + s // RING, s % RING, ws)
                    if s < RING:
                        following = slots_of(t + 1)
                    else:
                        pe.reg_mov(next_code, pe.value_load(tile_i[0:1, 1, ds(t + 1, 1)], min_val=0, max_val=RING * RING - 1))
                    layer2(t - 1, s - 1, ws_before)
                    if s < RING:
                        tiles_from(i, s + 1, following)
                with pe.Else():
                    with pe.If(t < last + 1):
                        ws, ws_before = slots or parts_of(pe.snap(next_code, min_val=0, max_val=RING * RING - 1))
                        turn_h(t - 1, s - 1)
                        layer2(t - 1, s - 1, ws_before)

            turn(0, 0, 0)
            turn(1, 0, 1)
            ws, _ = slots_of(0)
            layer1(0, 0, 0, ws)
            next_code = pe.alloc_register("next_code")
            pe.reg_mov(next_code, pe.value_load(tile_i[0:1, 1, 1:2], min_val=0, max_val=RING * RING - 1))
            with pe.Fori(0, TLOOP // RING) as i:
                with pe.If(i * RING < last + 1):
                    tiles_from(i, 1, None)

            def over_nodes(ps, ready, a, done, halves=1):
                for g in range(NFG + 1):
                    q, b = group(g)
                    pe.wait_ge(ready, g + 1)
                    for i in range(b.start, b.stop if g == NFG else b.start + BPG // halves):
                        m = pe.matmul(ps, onesf[0:q, :], a[0:q, i, :], start=(i == 0), stop=(i == NB - 1), skip_group_check=True)
                m.then_inc(done, 1)

            over_nodes(sum_ps, y_summed, F, sum_done)
            over_nodes(sq_ps, sq_halved, squares, sq_done, 2)

        @block.vector
        def _(dve):
            dve.memset(bases_i[:, 0, :], 2 * NWT * P).then_inc(bases_set, 1)
            dve.memset(src_i[:, EC:EW], N)
            dve.memset(padends[:, 0, :], NOWHERE)
            dve.memset(padends[:, 1, :], N)
            dve.memset(G[:, NB - 1, D:2 * D], 0.0).then_inc(tails_set, 1)
            dve.memset(zeros[:, :], 0.0)
            dve.memset(onesf[:, :], 1.0)
            dve.memset(ones_b[:, :], 1.0)
            dve.memset(eps_c[:, :], EPS)
            dve.memset(before[:, :, :], 0.0)
            dve.memset(iota[:, :], 0.0)
            dve.wait_ge(iotas, 1)
            dve.drain()
            dve.tensor_copy(iota[:, 0:P], iota_i[:, :])
            dve.tensor_copy(pcol[:, :], pcol_i[:, :])
            dve.tensor_copy(first_w[:, :], win_i[:, :])
            dve.drain()
            for m in range(3):
                dve.tensor_scalar(below[:, m, :], first_w[:, :], m - 0.5, None, ALU.add)
            dve.tensor_scalar(iota[:, P:192], iota[:, 0:192 - P], float(P), None, ALU.add)
            dve.tensor_scalar(ident[:, :], iota[:, 0:P], pcol[:, :], None, ALU.is_equal)
            dve.tensor_scalar(tri, iota[:, 0:P], pcol[:, :], None, ALU.is_gt)
            dve.drain().then_inc(consts, 1)
            dve.sem_inc(prod_copied, 2)
            dve.sem_inc(evacuated, 2)
            dve.sem_inc(x_made, 2)
            dve.sem_inc(y_ready, 2)
            dve.sem_inc(tx_ready, 2)
            dve.sem_inc(h1_ready, 2 * HK)
            dve.sem_inc(hs_ready, 2)
            dve.tensor_copy(iota_lo16[:, :, :], iota[:, 0:P].unsqueeze(2).to_broadcast([P, P, HC]))
            dve.tensor_copy(iota_hi16[:, :, :], iota[:, 0:NB].unsqueeze(2).to_broadcast([P, NB, HC]))

            dve.wait_ge(bases_in, 16 * (rest + 2))
            dve.tensor_scalar(bases_i[:, 0, :], bases_i[:, 0, :], WN.bit_length() - 1, None, ALU.logical_shift_right)
            dve.drain()
            dve.tensor_scalar(bases_i[:, 1, :], bases_i[:, 0, :], P - 1, None, ALU.bitwise_and)
            dve.tensor_scalar(bases_i[:, 2, :], bases_i[:, 0, :], P.bit_length() - 1, None, ALU.logical_shift_right)
            dve.drain()
            dve.tensor_copy(base_f[:, :, :], bases_i[:, 1:3, :])
            dve.drain()
            for hot, m, n in ((base_lo, 0, P), (base_hi, 1, NWT)):
                dve.tensor_tensor(hot, base_f[:, m, :].unsqueeze(2).to_broadcast([P, RC, n]),
                                  iota[:, 0:n].unsqueeze(1).to_broadcast([P, RC, n]), ALU.is_equal)
            dve.drain().then_inc(bases_hot, 1)

            dve.wait_ge(src_in, 32)
            src_g = src_i.rearrange("p (g c) -> p g c", g=NHG)
            digit_g = digit_i.rearrange("p (g c) -> p g c", g=NHG)
            dve.tensor_scalar(digit_g, src_g, P - 1, None, ALU.bitwise_and)
            dve.wait_ge(binned, 1)
            dve.tensor_copy(bins, bins_ps)
            dve.drain().then_inc(bins_copied, 1)
            dve.tensor_copy(src_lo[:, :, :], digit_g)
            dve.wait_ge(bins_summed, 1)
            dve.tensor_copy(bin_sums, bin_ps.to_broadcast([NWT, P]))
            dve.drain().then_inc(sums_copied, 1)
            dve.tensor_scalar(digit_g, src_g, P.bit_length() - 1, None, ALU.logical_shift_right)
            dve.drain()
            dve.tensor_copy(src_hi[:, :, :], digit_g)
            dve.drain()
            dve.wait_ge(rows_counted, 1)
            dve.tensor_scalar(row_w[:, :], below_ps, -1.0, 0.0, ALU.add, ALU.max)
            dve.drain().then_inc(row_ready, 1)

            def count(g, s):
                dve.wait_ge(hist_used, g + 1)
                dve.tensor_tensor(hist_lo[s], src_lo[:, ds(g, 1), :].to_broadcast([P, P, HC]), iota_lo16[:, :, :], ALU.is_equal)
                dve.tensor_tensor(hist_hi[s], src_hi[:, ds(g, 1), :].to_broadcast([P, NB, HC]), iota_hi16[:, :, :], ALU.is_equal
                                  ).then_inc(hist_ready, 1)

            def count_pairs(first, end):
                with dve.Fori(first, end) as i:
                    for s in range(2):
                        count(i * 2 + s, s)

            count_pairs(0, 1)
            dve.wait_ge(weights_in, NW)
            dve.tensor_tensor(bias_x[:, 0, :], bias_x[:, 0, :], bias_x[:, 1, :], ALU.add)
            dve.drain().then_inc(bias_ready, 1)
            count_pairs(1, G_EDGE)
            dve.wait_ge(found_counted, 1)
            dve.tensor_scalar(signs[:, 0, :], row_w[:, :], float(ROW), ROW / 2.0, ALU.mult, ALU.add)
            dve.drain()
            dve.scalar_tensor_tensor(edge_w[:, :], signs[:, 1, :], 0.5, signs[:, 0, :], ALU.mult, ALU.add)
            dve.drain().then_inc(edge_ready, 1)
            count_pairs(G_EDGE, G_DIGITS)
            dve.tensor_copy(iota_lo[:, :, :], iota[:, 0:P].unsqueeze(2).to_broadcast([P, P, WB]))
            dve.tensor_copy(iota_v[:, :, :], iota[:, 0:WV].unsqueeze(2).to_broadcast([P, WV, WB]))
            dve.tensor_scalar(tri_b[:, :], iota[:, 0:P], pcol[:, :], None, ALU.is_gt)
            dve.tensor_scalar(tri_eq[:, :], iota[:, 0:P], pcol[:, :], None, ALU.is_ge)
            for m in range(4):
                dve.tensor_scalar(pcols[:, m:m + 1], pcol[:, :], float(WN), float(m % WN - (m // WN) * P), ALU.mult, ALU.add)
            dve.drain()
            for m in range(4):
                dve.tensor_scalar(pick[:, m, :], iota[:, 0:P], pcols[:, m:m + 1], 0.5, ALU.is_equal, ALU.mult)
            dve.wait_ge(window_counted, 1)
            dve.wait_ge(src_w_in, 16 * NWT)
            dve.tensor_scalar(hi_w, src_w, P.bit_length() - 1, None, ALU.logical_shift_right)
            dve.tensor_tensor(rel_w, dst_w, first_w[:, :].unsqueeze(2).to_broadcast([P, NWT, P]), ALU.subtract)
            dve.drain()
            dve.scalar_tensor_tensor(low_w, hi_w, float(-P), src_w, ALU.mult, ALU.add)
            dve.scalar_tensor_tensor(rel_w, rel_w, float(NB), hi_w, ALU.mult, ALU.add)
            dve.drain().then_inc(digits_ready, 1)
            dve.tensor_tensor(deg_w[:, :, :], signs[:, 3:5, :], signs[:, 2:4, :], ALU.subtract)
            dve.drain()
            dve.tensor_reduce(held[:, :], deg_w[:, :, :], AX.XY, ALU.add)
            dve.drain().then_inc(deg_ready, 1)
            count_pairs(G_DIGITS, G_DEG)
            dve.wait_ge(deg_placed, 1)
            dve.tensor_scalar(rs_in[:, :].rearrange("p (t h) -> p h t", h=2), small[:, 0:64].rearrange("p (h t) -> p h t", h=2)[:, :, 0:NWT],
                              1.0, None, ALU.max).then_inc(deg_clipped, 1)
            dve.tensor_scalar(general_f[:, :], small[0:1, 64:65], 2.0 * E, None, ALU.is_lt)
            dve.drain()
            dve.tensor_copy(general[:, :], general_f[:, :])
            dve.drain().then_inc(general_ready, 1)
            count_pairs(G_DEG, NHG // 2)
            count(NHG - 1, 0)
            is_general = dve.value_load(general[0:1, 0:1], min_val=0, max_val=1)
            dve.wait_ge(hist_done, 1)
            dve.tensor_scalar(degs[:, 0, :], hist_ps, 1.0, None, ALU.max).then_inc(deg_clipped, 1)

            def reciprocals():
                dve.wait_ge(deg_root, 2)
                dve.reciprocal(rs_in[:, :], rs_in[:, :])
                dve.reciprocal(rs_out[:, :], rs_out[:, :])
                dve.drain().then_inc(rs_ready, 1)

            def lower_part(j):
                dve.wait_ge(upper_ready, j + 1)
                for b in range(j * BLK7, (j + 1) * BLK7):
                    m = dve.scalar_tensor_tensor(parts[:, b, 0:D], G[:, b, 0:D], rs_out[:, b:b + 1], parts[:, b, D:2 * D].bitcast(F32),
                                                 ALU.mult, ALU.subtract)
                m.then_inc(split, 1)

            def one_hots(n, i):
                first = n * WPB + i * WB
                dve.wait_ge(built, n * BPB + (i + 1))
                dve.tensor_tensor(oh_lo[i % OHB], edge_lo[:, ds(first, WB)].unsqueeze(1).to_broadcast([P, P, WB]), iota_lo[:, :, :], ALU.is_equal)
                dve.tensor_tensor(oh_v[i % OHB], edge_v[:, ds(first, WB)].unsqueeze(1).to_broadcast([P, WV, WB]), iota_v[:, :, :], ALU.is_equal
                                  ).then_inc(onehot_ready, 1)

            dve.wait_ge(edges_ready, 2 * NTG)
            with dve.If(is_general > 0):
                reciprocals()
                for j in range(NPC):
                    lower_part(j)
                dve.drain()
                for j in range(NPC):
                    if j >= 2:
                        dve.wait_ge(piece_out[j % 2], 16 * (j // 2))
                    b = slice(j * BLK7, (j + 1) * BLK7)
                    dve.tensor_tensor(piece[j % 2], parts[:, b, 0:D].bitcast(F32), parts[:, b, D:2 * D].bitcast(F32), ALU.add
                                      ).then_inc(piece_ready, 1)
                for s in range(2):
                    dve.wait_ge(piece_out[s], 16 * sum(j % 2 == s for j in range(NPC)))
                dve.memset(slow_sums, 0.0)
                dve.memset(degs[:, 1, :], 0.0)
                dve.drain().then_inc(slow_used, 1)
                with dve.Fori(0, NSG) as g:
                    dve.wait_ge(slow_edges_in, g * 32 + 32)
                    dve.tensor_copy(slow_rel[:, :], slow_dst[:, :])
                    dve.drain()
                    with dve.Fori(0, NB) as b:
                        dve.tensor_tensor(slow_hot, slow_rel[:, :].unsqueeze(2).to_broadcast([P, SC, P]),
                                          iota[:, 0:P].unsqueeze(1).to_broadcast([P, SC, P]), ALU.is_equal).then_inc(slow_hot_ready, 1)
                        dve.wait_ge(slow_summed, g * NB + (b + 1))
                        sums_b = slow_sums[:, ds(b, 1), :].rearrange("p b d -> p (b d)")
                        dve.tensor_tensor(sums_b, sums_b, slow_ps[:, 0:D], ALU.add)
                        dve.tensor_tensor(degs[:, 1, ds(b, 1)], degs[:, 1, ds(b, 1)], slow_ps[:, D:D + 1], ALU.add)
                        dve.tensor_scalar(slow_rel[:, :], slow_rel[:, :], float(-P), None, ALU.add)
                        dve.drain()
                    dve.drain().then_inc(slow_used, 1)
                dve.tensor_scalar(degs[:, 1, :], degs[:, 1, :], 1.0, None, ALU.max).then_inc(deg_clipped, 1)
                dve.wait_ge(deg_root, 3)
                dve.reciprocal(rs_in[:, 0:NB], rs_in[:, 0:NB])
                dve.drain()
                with dve.Fori(0, NB) as b:
                    dve.wait_ge(slow_res_in, b * 16 + 16)
                    dve.scalar_tensor_tensor(fblk, slow_sums[:, ds(b, 1), :].rearrange("p b d -> p (b d)"), rs_in[:, ds(b, 1)], fblk,
                                             ALU.mult, ALU.add).then_inc(slow_added, 1)
                dve.memset(edge_v, -1.0)
                dve.drain()
                for i in range(BPB):
                    one_hots(0, i)
                for i in range(OHB):
                    one_hots(1, i)
            with dve.Else():
                for i in range(BPB):
                    one_hots(0, i)
                    if i == 1:
                        reciprocals()
                    if i >= OHB:
                        lower_part(i - OHB)
                for j in range(BPB - OHB, NPC):
                    lower_part(j)
                    if j < BPB - OHB + 2:
                        for i in range(2):
                            one_hots(1, (j - (BPB - OHB)) * 2 + i)

            def make_x(n, j, s, h, half):
                dve.wait_ge(summed, n + 3)
                dve.wait_ge(res_in[s], half * 16 + 16)
                if not isinstance(j, int) or j >= 2:
                    dve.wait_ge(x_out[s], half * 16)
                at, rs = pair_x[s][:, h, :], rs_in[:, ds(n, 1)]
                dve.scalar_tensor_tensor(at, agg_ps[h][:, 0:D], rs, res_buf[s][:, h, :], ALU.mult, ALU.add)
                dve.drain()
                dve.scalar_tensor_tensor(at, agg_ps[h][:, D:2 * D], rs, at, ALU.mult, ALU.add).then_inc(x_made, 1)

            def choose(j, s, nb, valid):
                dve.wait_ge(logits_done, j + 1)
                dve.tensor_tensor(logit[:, 0:nb], logit_ps[:, 0:nb], bg_s[:, :].unsqueeze(1).to_broadcast([P, nb, NEXP]), ALU.add)
                dve.drain()
                for b in range(nb):
                    dve.max(top8[:, b, :], logit[:, b, :])
                dve.drain()
                for b in range(nb):
                    dve.max_index(top8i[:, b, :], top8[:, b, :], logit[:, b, :])
                dve.tensor_tensor(gap[:, s, 0:nb], top8[:, 0:nb, 1], top8[:, 0:nb, 0], ALU.subtract).then_inc(gap_ready, 1)
                dve.drain()
                dve.tensor_copy(expert[:, s, 0:nb], top8i[:, 0:nb, 0:2])
                dve.drain()
                for b in range(nb):
                    dve.tensor_tensor(picks[:, s, b], expert[:, s, b].unsqueeze(2).to_broadcast([P, 2, NEXP]),
                                      iota[:, 0:NEXP].unsqueeze(1).to_broadcast([P, 2, NEXP]), ALU.is_equal)
                dve.drain()
                dve.tensor_tensor(both[:, s, 0:nb], picks[:, s, 0:nb, 0], picks[:, s, 0:nb, 1], ALU.add)
                dve.drain().then_inc(both_ready, 1)
                if not isinstance(j, int) or j > 0:
                    dve.wait_ge(ranks_done, j)
                dve.tensor_copy(before[:, 1 - s, :], before[:, s, :])
                dve.drain()
                dve.tensor_tensor(before[0:valid, 1 - s, :], before[0:valid, 1 - s, :], both[0:valid, s, 0, :], ALU.add)
                if nb == 2:
                    dve.drain()
                    dve.tensor_tensor(before[:, 1 - s, :], before[:, 1 - s, :], both[:, s, 1, :], ALU.add)

            def place(j, s, nb):
                dve.wait_ge(ranks_done, j + 1)
                for b in range(nb):
                    dve.tensor_tensor(ranked[:, b], picks[:, s, b], rank_ps[:, b, :].unsqueeze(1).to_broadcast([P, 2, NEXP]), ALU.mult)
                dve.drain()
                dve.tensor_reduce(rank[:, 0:nb], ranked[:, 0:nb], AX.X, ALU.add)
                dve.drain()
                dve.tensor_scalar(over[:, 0:nb], rank[:, 0:nb], float(CAP), float(NSLOT), ALU.is_ge, ALU.mult)
                dve.scalar_tensor_tensor(slot_f[:, 0:nb], expert[:, s, 0:nb], float(LROWS), rank[:, 0:nb], ALU.mult, ALU.add)
                dve.wait_ge(egap_ready, j + 1)
                dve.tensor_scalar(gap[:, s, 0:nb], egap[:, s, 0:nb], 1.0, None, ALU.add)
                dve.drain()
                if not isinstance(j, int) or j >= 2:
                    dve.wait_ge(list_out[s], list_before(j, s))
                dve.tensor_tensor(slot[:, s, 0:nb], slot_f[:, 0:nb], over[:, 0:nb], ALU.add)
                gates = entry[:, s, 0:nb, :, 2].bitcast(F32)
                dve.reciprocal(gates[:, :, 0], gap[:, s, 0:nb])
                dve.drain()
                dve.tensor_tensor(gates[:, :, 1], gates[:, :, 0], egap[:, s, 0:nb], ALU.mult)
                dve.tensor_copy(entry[:, s, 0:nb, :, 0:2].rearrange("p b k c -> p (b k) c"),
                                tok_view(j, nb))
                dve.drain().then_inc(slots_ready, 1)

            def tok_view(j, nb):
                return tok_i[:, ds(j * 2, nb), :, :].rearrange("p b k c -> p (b k) c")

            def list_before(j, s):
                n = (j - s) // 2 if isinstance(j, int) else j_half[0]
                return n * 64

            j_half = [0]

            def step(j, s, half):
                after, first = j - 1, isinstance(j, int) and j == 0
                half_after = after // 2 if isinstance(j, int) else (half if s == 1 else half - 1)
                if not first:
                    make_x(j * 2 - 1, after, 1 - s, 1, half_after)
                for i in range(4, 6):
                    one_hots(j * 2 + 1, i)
                if not first:
                    choose(after, 1 - s, 2, P)
                for i in range(6, 8):
                    one_hots(j * 2 + 1, i)
                for i in range(0, 2):
                    one_hots(j * 2 + 2, i)
                make_x(j * 2, j, s, 0, j // 2 if isinstance(j, int) else half)
                for i in range(2, 6):
                    one_hots(j * 2 + 2, i)
                if not first:
                    j_half[0] = half_after
                    place(after, 1 - s, 2)
                for i in range(6, 8):
                    one_hots(j * 2 + 2, i)
                if not isinstance(j, int) or j < NPAIR - 1:
                    for i in range(4):
                        one_hots(j * 2 + 3, i)

            dve.wait_ge(iotas, 2)
            dve.memset(entry[:, :, :, :, :], 0)
            for j in range(2):
                step(j, j, None)
            with dve.Fori(1, NPAIR // 2 - 1) as i:
                for s in range(2):
                    step(i * 2 + s, s, i)
            for j in range(NPAIR - 2, NPAIR):
                step(j, j % 2, None)
            make_x(NB - 2, NPAIR - 1, (NPAIR - 1) % 2, 1, (NPAIR - 1) // 2)
            choose(NPAIR - 1, (NPAIR - 1) % 2, 2, P)
            make_x(NB - 1, NPAIR, NPAIR % 2, 0, NPAIR // 2)
            place(NPAIR - 1, (NPAIR - 1) % 2, 2)
            choose(NPAIR, NPAIR % 2, 1, TAIL)
            place(NPAIR, NPAIR % 2, 1)

            dve.drain().then_inc(tables_col, 1)
            dve.wait_ge(tables, 1)
            dve.tensor_scalar(cntc[:, 0:1], small[0:NEXP, 0:1], float(CAP), float(P - 1), ALU.min, ALU.add)
            dve.drain()
            dve.tensor_copy(cnti[:, 0:1], cntc[:, 0:1])
            dve.drain()
            dve.tensor_scalar(cnti[:, 1:2], cnti[:, 0:1], P.bit_length() - 1, None, ALU.logical_shift_right)
            dve.drain()
            dve.tensor_copy(cntc[:, 1:2], cnti[:, 1:2])
            dve.drain()
            dve.tensor_scalar(cntc[:, 3:4], cntc[:, 1:2], 0.0, None, ALU.is_gt)
            dve.drain().then_inc(tables_col, 1)
            dve.wait_ge(tables, 2)
            dve.tensor_copy(cntc[:, 2:3], bank[2][0:NEXP, 0:1])
            dve.drain()
            dve.tensor_scalar(ended[:, :], iota[0:NEXP, :], cntc[:, 2:3], None, ALU.is_ge)
            dve.drain().then_inc(tables_col, 1)
            dve.wait_ge(tables, 3)
            T = slice(0, TMAX)
            dve.tensor_tensor(tile_f[:, 0, T], iota[0:1, T], bank[3][0:1, T], ALU.subtract)
            dve.tensor_copy(tile_i[:, 1, T], bank[5][0:1, T])
            dve.drain()
            dve.tensor_scalar(tile_i[:, 1, T], tile_i[:, 1, T], RING - 1, None, ALU.bitwise_and)
            dve.scalar_tensor_tensor(tile_f[:, 1, T], tile_f[:, 0, T], float(NEXP), bank[2][0:1, T], ALU.mult, ALU.add)
            dve.drain()
            dve.tensor_copy(tile_f[:, 2, T], tile_i[:, 1, T])
            dve.drain()
            dve.scalar_tensor_tensor(tile_f[:, 3, T], tile_f[:, 1, T], float(RING), tile_f[:, 2, T], ALU.mult, ALU.add)
            dve.drain()
            dve.tensor_copy(tile_i[:, 0, T], tile_f[:, 3, T])
            dve.scalar_tensor_tensor(tile_f[:, 0, 1:TMAX], tile_f[:, 2, 0:TMAX - 1], float(RING), tile_f[:, 2, 1:TMAX], ALU.mult, ALU.add)
            dve.tensor_copy(tile_f[:, 0, 0:1], tile_f[:, 2, 0:1])
            dve.drain()
            dve.tensor_copy(tile_i[:, 1, T], tile_f[:, 0, T])
            dve.tensor_copy(last_i[:, :], bank[6][0:1, 0:1])
            dve.drain().then_inc(tiles_ready, 1)

            dve.drain()
            last = dve.value_load(last_i[0:1, 0:1], min_val=1, max_val=TMAX)

            def copy_h(t, s):
                dve.wait_ge(hT_done, t + 1)
                dve.wait_ge(h_done, t + 3)
                dve.tensor_copy(hs[:, s % 2, :], h_ps[s % 2][:, :]).then_inc(hs_ready, 1)

            def result(t, i, s):
                code = dve.value_load(tile_i[0:1, 0, ds(t, 1)], min_val=0, max_val=(8 * NEXP * RING) - 1)
                ws = dve.snap(code & (RING - 1))
                dve.wait_ge(y_out[s], i * 16 + 16)
                dve.wait_ge(tile_done, t + (RING + 1))
                dve.tensor_tensor(yo[:, s, :], y_ps[s % 2], b2s[:, ds(ws, 1), :].rearrange("p s d -> p (s d)"), ALU.add)
                dve.drain()
                dve.tensor_scalar(yo[:, s, :], yo[:, s, :], lt[:, s, 2:3].bitcast(F32), None, ALU.mult).then_inc(y_ready, 1)

            copy_h(0, 0)
            with dve.Fori(0, TLOOP // RING) as i:
                with dve.If(i * RING < last + 1):
                    for s in range(1, RING + 1):
                        t = i * RING + s
                        with dve.If(t < last):
                            copy_h(t, s)
                            result(t - 1, i, s - 1)
                        with dve.Else():
                            with dve.If(t < last + 1):
                                result(t - 1, i, s - 1)

            dve.wait_ge(x_in, 16 * NPC)
            for g in range(NFG + 1):
                q, b = group(g)
                dve.wait_ge(y_in[g], 16)
                dve.tensor_tensor(F[0:q, b], F[0:q, b], results[g][0:q, :, 0], ALU.add)
                dve.drain()
                dve.tensor_tensor(F[0:q, b], F[0:q, b], results[g][0:q, :, 1], ALU.add).then_inc(y_summed, 1)
            dve.wait_ge(sum_done, 1)
            dve.tensor_scalar(mean[:, :], sum_ps, 1.0 / N, None, ALU.mult)
            dve.drain()

            def halve(g):
                dve.wait_ge(squared, g + 1)
                if g < NFG:
                    b, h = g * BPG, BPG // 2
                    dve.tensor_tensor(squares[:, b:b + h], squares[:, b:b + h], squares[:, b + h:b + 2 * h], ALU.add).then_inc(sq_halved, 1)
                else:
                    dve.drain().then_inc(sq_halved, 1)

            for g in range(NFG + 1):
                q, b = group(g)
                dve.tensor_tensor(F[0:q, b], F[0:q, b], mean[0:q, :].unsqueeze(1).to_broadcast(list(F[0:q, b].shape)), ALU.subtract).then_inc(centred, 1)
                if g > 0:
                    halve(g - 1)
            halve(NFG)
            dve.wait_ge(sq_done, 1)
            dve.tensor_scalar(mean[:, :], sq_ps, 1.0 / N, None, ALU.mult).then_inc(var_ready, 1)
            dve.wait_ge(root_ready, 1)
            dve.reciprocal(scale[:, :], scale[:, :])
            dve.drain()
            dve.tensor_tensor(scale[:, :], scale[:, :], gb_s[:, 0, :], ALU.mult).then_inc(scale_ready, 1)

            def invert(g):
                q, b = group(g)
                n, r, sh = b.stop - b.start, inv[0:q, g % 2], shift[0:q, g % 2]
                dve.wait_ge(lnroot_ready, g + 1)
                dve.reciprocal(r[:, 0:n], r[:, 0:n])
                dve.drain()
                dve.scalar_tensor_tensor(sh[:, 0:n], moments[0:q, g % 2, 0:n, 0], -1.0, r[:, 0:n], ALU.mult, ALU.mult)
                dve.drain().then_inc(shift_ready, 1)

            for g in range(NFG + 1):
                q, b = group(g)
                n = b.stop - b.start
                dve.wait_ge(f_ready, g + 1)
                if g == 0:
                    dve.drain()
                    dve.tensor_tensor(F[0:q, b], F[0:q, b], scale[0:q, :].unsqueeze(1).to_broadcast(list(F[0:q, b].shape)), ALU.mult)
                    dve.drain()
                else:
                    dve.wait_ge(scaled, g)
                dve.tensor_tensor(F[0:q, b], F[0:q, b], feats[0:q, b], ALU.add)
                dve.drain()
                for i in range(n):
                    dve.bn_stats(stats[0:q, i, :], F[0:q, b.start + i, :])
                if g > 0:
                    invert(g - 1)
                if g >= 2:
                    dve.wait_ge(out_ready, g - 1)
                dve.drain()
                for i in range(n):
                    dve.bn_aggr(moments[0:q, g % 2, i, :], stats[0:q, i, :])
                dve.drain().then_inc(lnvar_ready, 1)
            invert(NFG)


_INS = ["x", "src", "dst", "L0_gnn_W_gc", "L0_gnn_b_gc", "L0_gnn_W_res", "L0_gnn_b_res", "L0_gnn_Wg", "L0_gnn_bg",
        "L0_gnn_w1", "L0_gnn_b1", "L0_gnn_w2", "L0_gnn_b2", "L0_gnn_gamma", "L0_gnn_beta"]


def kernel(**inputs):
    import numpy as _np
    import concourse.bacc as _bacc
    from concourse import mybir as _mybir
    from concourse.bass_utils import run_bass_kernel_spmd as _run

    nc = _bacc.Bacc("TRN2", target_bir_lowering=False, num_devices=1)
    arrays, args = {}, []
    for name in _INS:
        a = _np.ascontiguousarray(inputs[name])
        arrays[f"in_{name}_dram"] = a
        args.append(nc.dram_tensor(f"in_{name}_dram", a.shape, _mybir.dt.from_np(a.dtype), kind="ExternalInput").ap())
    shape = inputs["x"].shape
    args.append(nc.dram_tensor("out_0_dram", shape, _mybir.dt.float32, kind="ExternalOutput").ap())
    gnn_kernel(nc, *args)
    r = _run(nc, [arrays], core_ids=[0])
    return r.results[0]["out_0_dram"]
```
